# Optimizing a Trainium2 kernel written in Bass

```python
import numpy as np
import jax
import jax.numpy as jnp

def _softmax(x, axis=-1):
    return jax.nn.softmax(x, axis=axis)

def _gelu(x):
    return jax.nn.gelu(x, approximate=True)

def _silu(x):
    return jax.nn.silu(x)

def _sigmoid(x):
    return jax.nn.sigmoid(x)

def _layernorm(x, axis=-1, eps=1e-05):
    m = jnp.mean(x, axis=axis, keepdims=True)
    v = jnp.var(x, axis=axis, keepdims=True)
    return (x - m) / jnp.sqrt(v + eps)

def _scatter_add(tgt, idx, src, axis=0):
    return tgt.at[idx].add(src)

def _segment_sum(src, seg, n):
    return jax.ops.segment_sum(src, seg, n)
kernel_name = 'mk_recurrent_d2_jaxref_r8_5fe01c'

def setup_inputs(seed: int=0):
    np.random.seed(seed)
    _w = jnp.asarray

    def _L0_attn_setup():
        import jax, jax.numpy as jnp
        import numpy as np
        import math
        CTX_LEN = 96
        N_EMBD = 128

        def _depthwise_causal_conv(z, w, T, C):
            return jax.lax.conv_general_dilated(z, w, window_strides=(1,), padding=[(T - 1, 0)], feature_group_count=C, dimension_numbers=('NCH', 'OIH', 'NCH'))
        key = jax.random.key(seed)
        ks = jax.random.split(key, 8)
        B, T, C = (8, CTX_LEN, N_EMBD)
        x = jax.random.normal(ks[0], (B, T, C), dtype=jnp.float32)
        time_decay = jax.random.normal(ks[1], (C, 1), dtype=jnp.float32) * 0.1
        time_first = jnp.full((C, 1), math.log(0.3), dtype=jnp.float32)
        time_mix = jax.random.uniform(ks[2], (1, 1, C), dtype=jnp.float32)
        s = 0.02
        Wk = jax.random.normal(ks[3], (C, C), dtype=jnp.float32) * s
        Wv = jax.random.normal(ks[4], (C, C), dtype=jnp.float32) * s
        Wr = jax.random.normal(ks[5], (C, C), dtype=jnp.float32) * s
        Wo = jax.random.normal(ks[6], (C, C), dtype=jnp.float32) * s
        return {'x': x, 'time_decay': time_decay, 'time_first': time_first, 'time_mix': time_mix, 'Wk': Wk, 'Wv': Wv, 'Wr': Wr, 'Wo': Wo}
    _L0_attn_in = _L0_attn_setup()

    def _L0_ffn_setup():
        import jax, jax.numpy as jnp
        import numpy as np
        import math
        D_IN = 128
        FEATURES = (512, 512, 128)
        BATCH, SEQ = (8, 256)

        def _conn_dense(kernel_bool, x):
            w = jnp.where(kernel_bool, jnp.float32(1.0), jnp.float32(-1.0))
            return x @ w
        key = jax.random.key(seed)
        kx, kk0, kk1, kk2 = jax.random.split(key, 4)
        x = jax.random.normal(kx, (BATCH, SEQ, D_IN), dtype=jnp.float32)
        k0 = jax.random.randint(kk0, (2 * D_IN, FEATURES[0]), 0, 2).astype(jnp.bool_)
        k1 = jax.random.randint(kk1, (FEATURES[0], FEATURES[1]), 0, 2).astype(jnp.bool_)
        k2 = jax.random.randint(kk2, (FEATURES[1], FEATURES[2]), 0, 2).astype(jnp.bool_)
        s0 = jnp.asarray(1.0 / math.sqrt(2 * D_IN), dtype=jnp.float32)
        s1 = jnp.asarray(1.0 / math.sqrt(FEATURES[0]), dtype=jnp.float32)
        s2 = jnp.asarray(1.0 / math.sqrt(FEATURES[1]), dtype=jnp.float32)
        return {'x': x, 'k0': k0, 'k1': k1, 'k2': k2, 's0': s0, 's1': s1, 's2': s2}
    _L0_ffn_in = _L0_ffn_setup()

    def _L1_attn_setup():
        import jax, jax.numpy as jnp
        import numpy as np
        D_MODEL = 128
        D_STATE = 16
        D_CONV = 4
        D_INNER = 2 * D_MODEL
        BATCH = 2
        SEQ = 256
        key = jax.random.key(seed)
        ks = jax.random.split(key, 8)
        s = 0.02
        return {'x': jax.random.normal(ks[0], (BATCH, SEQ, D_MODEL), jnp.float32), 'W_in': jax.random.normal(ks[1], (D_MODEL, 2 * D_INNER), jnp.float32) * s, 'conv_w': jax.random.normal(ks[2], (D_INNER, 1, D_CONV), jnp.float32) * s, 'conv_b': jnp.zeros((D_INNER,), jnp.float32), 'W_x': jax.random.normal(ks[3], (D_INNER, 2 * D_STATE + D_INNER), jnp.float32) * s, 'W_dt': jax.random.normal(ks[4], (D_STATE, D_INNER), jnp.float32) * s, 'b_dt': jnp.zeros((D_INNER,), jnp.float32), 'W_out': jax.random.normal(ks[5], (D_INNER, D_MODEL), jnp.float32) * s}
    _L1_attn_in = _L1_attn_setup()

    def _L1_ffn_setup():
        import jax, jax.numpy as jnp
        import numpy as np
        H_DIM, E_DIM = (128, 64)
        N_SHARED, N_ROUTED, TOP_K = (2, 16, 4)
        B, S = (4, 256)
        key = jax.random.key(seed)
        ks = jax.random.split(key, 6)
        sc = 1.0 / np.sqrt(H_DIM)
        ec = 1.0 / np.sqrt(E_DIM)
        return {'x': jax.random.normal(ks[0], (B, S, H_DIM), dtype=jnp.float32), 'shared_up': jax.random.uniform(ks[1], (N_SHARED, E_DIM, H_DIM), jnp.float32, -sc, sc), 'shared_down': jax.random.uniform(ks[2], (N_SHARED, H_DIM, E_DIM), jnp.float32, -ec, ec), 'routed_up': jax.random.uniform(ks[3], (N_ROUTED, E_DIM, H_DIM), jnp.float32, -sc, sc), 'routed_down': jax.random.uniform(ks[4], (N_ROUTED, H_DIM, E_DIM), jnp.float32, -ec, ec), 'router_w': jax.random.uniform(ks[5], (N_ROUTED, H_DIM), jnp.float32, -sc, sc)}
    _L1_ffn_in = _L1_ffn_setup()
    _d = {'L0_attn_x': _L0_attn_in['x'], 'L0_attn_time_decay': _L0_attn_in['time_decay'], 'L0_attn_time_first': _L0_attn_in['time_first'], 'L0_attn_time_mix': _L0_attn_in['time_mix'], 'L0_attn_Wk': _L0_attn_in['Wk'], 'L0_attn_Wv': _L0_attn_in['Wv'], 'L0_attn_Wr': _L0_attn_in['Wr'], 'L0_attn_Wo': _L0_attn_in['Wo'], 'L0_ffn_k0': _L0_ffn_in['k0'], 'L0_ffn_k1': _L0_ffn_in['k1'], 'L0_ffn_k2': _L0_ffn_in['k2'], 'L0_ffn_s0': _L0_ffn_in['s0'], 'L0_ffn_s1': _L0_ffn_in['s1'], 'L0_ffn_s2': _L0_ffn_in['s2'], 'L1_attn_W_in': _L1_attn_in['W_in'], 'L1_attn_conv_w': _L1_attn_in['conv_w'], 'L1_attn_conv_b': _L1_attn_in['conv_b'], 'L1_attn_W_x': _L1_attn_in['W_x'], 'L1_attn_W_dt': _L1_attn_in['W_dt'], 'L1_attn_b_dt': _L1_attn_in['b_dt'], 'L1_attn_W_out': _L1_attn_in['W_out'], 'L1_ffn_shared_up': _L1_ffn_in['shared_up'], 'L1_ffn_shared_down': _L1_ffn_in['shared_down'], 'L1_ffn_routed_up': _L1_ffn_in['routed_up'], 'L1_ffn_routed_down': _L1_ffn_in['routed_down'], 'L1_ffn_router_w': _L1_ffn_in['router_w']}
    _x0 = _d['L0_attn_x']
    _d['L0_attn_x'] = jax.random.normal(jax.random.fold_in(jax.random.key(seed), 1), (32, 256, 128), dtype=_x0.dtype)
    del _x0
    return _d

def reference(L0_attn_x, L0_attn_time_decay, L0_attn_time_first, L0_attn_time_mix, L0_attn_Wk, L0_attn_Wv, L0_attn_Wr, L0_attn_Wo, L0_ffn_k0, L0_ffn_k1, L0_ffn_k2, L0_ffn_s0, L0_ffn_s1, L0_ffn_s2, L1_attn_W_in, L1_attn_conv_w, L1_attn_conv_b, L1_attn_W_x, L1_attn_W_dt, L1_attn_b_dt, L1_attn_W_out, L1_ffn_shared_up, L1_ffn_shared_down, L1_ffn_routed_up, L1_ffn_routed_down, L1_ffn_router_w):

    def _L0_attn_ref(x, time_decay, time_first, time_mix, Wk, Wv, Wr, Wo):
        import jax, jax.numpy as jnp
        import numpy as np
        import math
        CTX_LEN = 96
        N_EMBD = 128

        def _depthwise_causal_conv(z, w, T, C):
            return jax.lax.conv_general_dilated(z, w, window_strides=(1,), padding=[(T - 1, 0)], feature_group_count=C, dimension_numbers=('NCH', 'OIH', 'NCH'))
        B, T, C = x.shape
        xs = jnp.pad(x, ((0, 0), (1, 0), (0, 0)))[:, :-1]
        xm = x * time_mix + xs * (1.0 - time_mix)
        k = jnp.einsum('btc,dc->bdt', xm, Wk)
        v = jnp.einsum('btc,dc->bdt', xm, Wv)
        r = jnp.einsum('btc,dc->btd', xm, Wr)
        k = jnp.exp(jnp.minimum(k, 60.0))
        kv = k * v
        time_curve = (jnp.arange(T - 1, dtype=jnp.float32) - (T - 2))[None, :]
        time_w = jnp.concatenate([jnp.exp(time_decay) * time_curve, time_first], axis=-1)
        w = jnp.exp(time_w)[:, None, :]
        wkv = _depthwise_causal_conv(kv, w, T, C)
        wk = _depthwise_causal_conv(k, w, T, C) + 1e-09
        rwkv = jax.nn.sigmoid(r) * jnp.swapaxes(wkv / wk, 1, 2)
        return jnp.einsum('btc,dc->btd', rwkv, Wo)

    def _L0_ffn_ref(x, k0, k1, k2, s0, s1, s2):
        import jax, jax.numpy as jnp
        import numpy as np
        import math
        D_IN = 128
        FEATURES = (512, 512, 128)
        BATCH, SEQ = (8, 256)

        def _conn_dense(kernel_bool, x):
            w = jnp.where(kernel_bool, jnp.float32(1.0), jnp.float32(-1.0))
            return x @ w
        h = jnp.concatenate([x, -x], axis=-1)
        h = s0 * _conn_dense(k0, h)
        h = jax.nn.relu(h) * 2
        h = s1 * _conn_dense(k1, h)
        h = jax.nn.relu(h) * 2
        h = s2 * _conn_dense(k2, h)
        return h

    def _L1_attn_ref(x, W_in, conv_w, conv_b, W_x, W_dt, b_dt, W_out):
        import jax, jax.numpy as jnp
        import numpy as np
        D_MODEL = 128
        D_STATE = 16
        D_CONV = 4
        D_INNER = 2 * D_MODEL
        BATCH = 2
        SEQ = 256
        b, s, _ = x.shape
        xr = x @ W_in
        x_in, res = (xr[..., :D_INNER], xr[..., D_INNER:])
        xc = jax.lax.conv_general_dilated(x_in.transpose(0, 2, 1), conv_w, window_strides=(1,), padding=[(D_CONV - 1, 0)], dimension_numbers=('NCH', 'OIH', 'NCH'), feature_group_count=D_INNER)
        xc = (xc + conv_b[None, :, None]).transpose(0, 2, 1)
        xc = jax.nn.silu(xc)
        p = xc @ W_x
        delta = jax.nn.softplus(p[..., :D_STATE] @ W_dt + b_dt)
        Bm = p[..., D_STATE:2 * D_STATE]
        Cm = p[..., 2 * D_STATE:]

        def step(h, inp):
            x_t, d_t, B_t, C_t = inp
            h = h * d_t[:, None, :] + B_t[:, :, None] * x_t[:, None, :]
            return (h, h.sum(axis=1) * C_t)
        h0 = jnp.zeros((b, D_STATE, D_INNER), x.dtype)
        xs = (xc.transpose(1, 0, 2), delta.transpose(1, 0, 2), Bm.transpose(1, 0, 2), Cm.transpose(1, 0, 2))
        _, ys = jax.lax.scan(step, h0, xs)
        y = ys.transpose(1, 0, 2) * jax.nn.silu(res)
        return y @ W_out

    def _L1_ffn_ref(x, shared_up, shared_down, routed_up, routed_down, router_w):
        import jax, jax.numpy as jnp
        import numpy as np
        H_DIM, E_DIM = (128, 64)
        N_SHARED, N_ROUTED, TOP_K = (2, 16, 4)
        B, S = (4, 256)
        b, s, h = x.shape
        xt = x.reshape(-1, h)
        up_s = jnp.einsum('th,seh->tse', xt, shared_up)
        shared = jnp.einsum('tse,she->th', jax.nn.gelu(up_s, approximate=False), shared_down)
        probs = jax.nn.softmax(xt @ router_w.T, axis=-1)
        topk_p, topk_i = jax.lax.top_k(probs, TOP_K)
        gate = jnp.zeros_like(probs).at[jnp.arange(xt.shape[0])[:, None], topk_i].add(topk_p)
        up_r = jnp.einsum('th,reh->tre', xt, routed_up)
        act = jax.nn.gelu(up_r, approximate=False) * gate[:, :, None]
        routed = jnp.einsum('tre,rhe->th', act, routed_down)
        return (shared + routed).reshape(b, s, h)
    x = L0_attn_x
    xn = _layernorm(x, axis=-1)
    s = _L0_attn_ref(xn, L0_attn_time_decay, L0_attn_time_first, L0_attn_time_mix, L0_attn_Wk, L0_attn_Wv, L0_attn_Wr, L0_attn_Wo)
    g = _silu(_L0_ffn_ref(xn, L0_ffn_k0, L0_ffn_k1, L0_ffn_k2, L0_ffn_s0, L0_ffn_s1, L0_ffn_s2))
    x = x + s * g
    xn = _layernorm(x, axis=-1)
    s = _L1_attn_ref(xn, L1_attn_W_in, L1_attn_conv_w, L1_attn_conv_b, L1_attn_W_x, L1_attn_W_dt, L1_attn_b_dt, L1_attn_W_out)
    g = _silu(_L1_ffn_ref(xn, L1_ffn_shared_up, L1_ffn_shared_down, L1_ffn_routed_up, L1_ffn_routed_down, L1_ffn_router_w))
    x = x + s * g
    return x

_drawn_inputs = setup_inputs


def setup_inputs(seed=0):
    import zlib

    import numpy as np

    out = dict(_drawn_inputs(seed))
    spreads = {'L0_attn_time_first': (-1.2039728164672852, 0.2),
     'L1_attn_conv_b': (0.0, 0.1),
     'L1_attn_b_dt': (0.0, 0.1)}
    factors = {}
    for name, (base, spread) in spreads.items():
        noise = np.random.default_rng([zlib.crc32(name.encode()), seed]).standard_normal(out[name].shape)
        drawn = base * np.exp(spread * noise) if base else spread * noise
        out[name] = jnp.asarray(drawn.astype(out[name].dtype))
    for name, factor in factors.items():
        out[name] = (out[name] * factor).astype(out[name].dtype)
    return out
```

```python
from contextlib import ExitStack
import math

import concourse.bass as bass
from concourse import mybir

ALU = mybir.AluOpType
ACT = mybir.ActivationFunctionType
AX = mybir.AxisListType
F32 = mybir.dt.float32
F16 = mybir.dt.float16
BF16 = mybir.dt.bfloat16
U8 = mybir.dt.uint8

P = 128
EPS = 1e-5
ARENA = 21 * 1024
WK_EPS = 1e-9
K_CAP = 60.0
SP_CAP = 30.0
XS = 2.0 ** 11
W0S = 2.0 ** -4
W1S = 2.0 ** -9
FS = 4.0 * 2.0 ** 2

SEM_NAMES = """
x_loaded w_loaded ident_ready sel_ready const_ready
w0_split tr_done bn_done w_ready act_w_ready pool_w_ready sign_ready scal_ready scal_done wt_ready wdt_done
a_stat a_rstd0 a_rstd a_centred a_xn a_xnT a_xs a_xh a_xm a_xl a_k a_v a_r a_ek a_ekm a_kv a_scanK a_scanV a_wkc a_wk a_wkv
a_rec a_y a_thr a_y2 a_z a_hi a_lo a_s a_f a_thf a_gp a_sg a_sgT a_x1
b_stat b_rstd0 b_rstd b_centred b_xn b_xnT b_xc b_xin b_res b_rout b_xi b_u0 b_conv b_thu b_xc2 b_thr b_r2
b_mx b_lg b_pe b_sum b_rs b_top b_top2 b_rep b_gt b_gn b_g1 b_g2 b_g3 b_g4 b_g5 b_gtT b_gT
b_up b_act b_actg b_gate b_down b_d b_e b_em b_ln b_delta b_c b_cr b_b b_bx b_scan b_y b_s b_thf b_gp b_sg b_sgT b_out
stored
""".split()


def build(nc, A, out):
    B, T, C = A["L0_attn_x"].shape
    SEQ = 512 // T
    N = SEQ * T
    J = N // P
    G = B * T // N
    F = A["L0_ffn_k0"].shape[1]
    FC = F // P
    DI = A["L1_attn_W_in"].shape[1] // 2
    IC = DI // P
    DS = A["L1_attn_W_dt"].shape[0]
    TAPS = A["L1_attn_conv_w"].shape[2]
    NR, E, _ = A["L1_ffn_routed_up"].shape
    NS = A["L1_ffn_shared_up"].shape[0]
    TOP_K = 4
    UC = (NS + NR) * E // P
    RC = NR * E // P

    x_d = A["L0_attn_x"].rearrange("b t c -> (b t) c").rearrange("(g p j) c -> g p (j c)", p=P, j=J)
    out_d = out.rearrange("b t c -> (b t) c").rearrange("(g p j) c -> g p (j c)", p=P, j=J)

    with ExitStack() as ctx:
        def sb(name, shape, dt=F32):
            return ctx.enter_context(nc.sbuf_tensor(name, shape, dt))

        sem = {n: ctx.enter_context(nc.semaphore(n)) for n in SEM_NAMES}

        bank = [ctx.enter_context(nc.psum_tensor(f"bank{i}", [P, 512], F32)) for i in range(8)]

        x_all = sb("x_all", [P, G * N])
        ident = sb("ident", [P, P])
        identb = sb("identb", [P, P], BF16)
        ones = sb("ones", [P, P])
        neghalf = sb("neghalf", [P, J])
        epsc = sb("epsc", [P, J])
        sel = sb("sel", [3 * NR, RC, P], BF16)

        wsq = sb("wsq", [P, 4, P])
        k0_u = sb("k0_u", [P, 2, F], U8)
        k1_u = sb("k1_u", [P, FC, F], U8)
        k2_u = sb("k2_u", [P, FC, P], U8)
        scal = sb("scal", [P, 3])
        chan = sb("chan", [P, 3])
        w_in = sb("w_in", [P, 2 * DI])
        cw = sb("cw", [P, IC, TAPS])
        cb = sb("cb", [P, IC])
        bdt = sb("bdt", [P, IC])
        wx = sb("wx", [P, IC, 2 * DS + DI])
        wdt = sb("wdt", [DS, DI])
        w_out = sb("w_out", [P, IC, P])
        up_n = sb("up_n", [P, UC, P])
        dn_n = sb("dn_n", [P, UC, P])
        rw_n = sb("rw_n", [NR, P])

        wsqT = sb("wsqT", [P, 4, P])
        w0 = sb("w0", [P, F], F16)
        w0d = sb("w0d", [P, F])
        w1 = sb("w1", [P, FC, F], F16)
        w2 = sb("w2", [P, FC, P], F16)
        sg_ = sb("sg_", [P, 2])
        sab = sb("sab", [P, 2])
        w0c = sb("w0c", [P, 1])
        w1c = sb("w1c", [P, 2])
        c3 = sb("c3", [P, 4])
        tch = sb("tch", [P, 4])
        dec = sb("dec", [P, T])
        upT = sb("upT", [P, UC, P])
        dnT = sb("dnT", [P, UC, P])
        rwT = sb("rwT", [P, NR])
        wxsT = sb("wxsT", [DS, IC, P])
        wdel = sb("wdel", [P, IC, DI])
        wc = sb("wc", [P, IC, DI])
        wbs = sb("wbs", [P, IC])
        wb = sb("wb", [P, IC, P])

        st = sb("st", [P, J, 6])
        mv = sb("mv", [P, J, 2])
        ve = sb("ve", [P, J])
        rstd = sb("rstd", [P, J])
        xn = sb("xn", [P, J, P])

        loads = []

        def wload(dst, src):
            loads.append((dst, src))

        for i, n in enumerate(("Wk", "Wv", "Wr", "Wo")):
            wload(wsq[:, i, :], A["L0_attn_" + n])
        wload(chan[:, 0:1], A["L0_attn_time_decay"])
        wload(chan[:, 1:2], A["L0_attn_time_first"])
        wload(chan[:, 2:3], A["L0_attn_time_mix"].rearrange("a b c -> c (a b)"))
        wload(k0_u[:, :, :], A["L0_ffn_k0"].rearrange("(k p) f -> p k f", p=P))
        for i, n in enumerate(("s0", "s1", "s2")):
            wload(scal[:, i:i + 1], A["L0_ffn_" + n].partition_broadcast(P))
        wload(k1_u[:, :, :], A["L0_ffn_k1"].rearrange("(k p) f -> p k f", p=P))
        wload(k2_u[:, :, :], A["L0_ffn_k2"].rearrange("(k p) f -> p k f", p=P))
        wload(w_in[:, :], A["L1_attn_W_in"])
        wload(cw[:, :, :], A["L1_attn_conv_w"].rearrange("(k p) a t -> p k (a t)", p=P))
        wload(cb[:, :], A["L1_attn_conv_b"].rearrange("(k p) -> p k", p=P))
        wload(bdt[:, :], A["L1_attn_b_dt"].rearrange("(k p) -> p k", p=P))
        wload(wx[:, :, :], A["L1_attn_W_x"].rearrange("(k p) m -> p k m", p=P))
        wload(wdt[:, :], A["L1_attn_W_dt"])
        wload(w_out[:, :, :], A["L1_attn_W_out"].rearrange("(k p) m -> p k m", p=P))
        wload(up_n[:, 0, :], A["L1_ffn_shared_up"].rearrange("s e h -> (s e) h"))
        wload(up_n[:, 1:UC, :], A["L1_ffn_routed_up"].rearrange("(k r) e h -> (r e) k h", r=P // E))
        wload(dn_n[:, 0, :].rearrange("h (s e) -> h s e", e=E), A["L1_ffn_shared_down"].rearrange("s h e -> h s e"))
        wload(dn_n[:, 1:UC, :].rearrange("h k (r e) -> h (k r) e", e=E), A["L1_ffn_routed_down"].rearrange("r h e -> h r e"))
        wload(rw_n[:, :], A["L1_ffn_router_w"])
        W_ALL = 16 * len(loads)

        block = ctx.enter_context(nc.Block())

        def after(eng, semaphore, value):
            if not (isinstance(value, int) and value <= 0):
                eng.wait_ge(semaphore, value)

        def groups(eng, body, tail=None):
            body(0)
            with eng.Fori(1, G) as n:
                body(n)
            if tail:
                tail(G)

        def xs_of(n):
            return x_all[:, bass.ds(n * N, N)]

        b_T, b_K, b_V, b_RX, b_Z0, b_Z1, b_S, b_F = bank

        turns = [(wsq[:, i, :], wsqT[:, i, :], P) for i in range(4)]
        turns += [(up_n[:, c, :], upT[:, c, :], P) for c in range(UC)]
        turns += [(dn_n[:, c, :], dnT[:, c, :], P) for c in range(UC)]
        turns += [(rw_n[:, :], rwT[:, :], NR)]
        turns += [(wx[:, k, 0:DS], wxsT[:, k, :], P) for k in range(IC)]
        TB = 4

        arena = sb("arena", [P, ARENA])
        cut = {0: 0, 1: 0}

        def tile(layer, shape, dt=F32):
            size = math.prod(shape[1:]) * (2 if dt in (F16, BF16) else 4) // 4
            flat = arena[0:shape[0], cut[layer]:cut[layer] + size]
            cut[layer] += size
            assert cut[layer] <= ARENA
            flat = flat if dt == F32 else flat.bitcast(dt)
            names = "abcd"[:len(shape) - 1]
            if len(names) == 1:
                return flat
            return flat.rearrange(f"p ({' '.join(names)}) -> p {' '.join(names)}",
                                  **dict(zip(names, shape[1:])))

        if True:
            def t0(name, shape, dt=F32):
                return tile(0, shape, dt)

            def t1(name, shape, dt=F32):
                return tile(1, shape, dt)
            a_ = sb("a_", [P, SEQ, T])
            xm = t0("xm", [P, N])
            xh = t0("xh", [P, N], F16)
            xl = t0("xl", [P, N], F16)
            ek = t0("ek", [P, N])
            ekm = t0("ekm", [P, N])
            kv = t0("kv", [P, N])
            Pk = sb("Pk", [P, SEQ, T + 1])
            Pv = sb("Pv", [P, SEQ, T + 1])
            wkc = t0("wkc", [P, N])
            wk = t0("wk", [P, N])
            wkv = t0("wkv", [P, N])
            rec = t0("rec", [P, N])
            yq = t0("yq", [P, N])
            thr = t0("thr", [P, N])
            y2 = t0("y2", [P, N])
            hh = t0("hh", [P, 2, FC, N], F16)
            hl = t0("hl", [P, 2, FC, N], F16)
            thf = t0("thf", [P, N])
            gp = t0("gp", [P, N])
            sg = t0("sg", [P, N])
            thf1 = t1("thf1", [P, N])
            gp1 = t1("gp1", [P, N])
            sg1 = t1("sg1", [P, N])
            xc = t1("xc", [P, N])
            xi = sb("xi", [P, IC, SEQ, T + TAPS - 1])
            u = t1("u", [P, IC, N])
            thu = t1("thu", [P, IC, N])
            xc2 = t1("xc2", [P, IC, N])
            th2 = t1("th2", [P, IC, N])
            r2 = t1("r2", [P, IC, N])
            lg = t1("lg", [P, J, NR])
            mx = t1("mx", [P, J])
            pe_ = sb("pe_", [P, J, NR + TOP_K])
            sm = t1("sm", [P, J])
            rs = t1("rs", [P, J])
            top = t1("top", [P, J, 8])
            rep = t1("rep", [P, J, NR + TOP_K])
            gt = t1("gt", [P, J, NR])
            gn = t1("gn", [P, J, NR])
            gr1 = t1("gr1", [P, J, NR])
            gr2 = t1("gr2", [P, J, NR])
            g3 = t1("g3", [P, J, 3, NR], BF16)
            gT = t1("gT", [3 * NR, N], BF16)
            act = t1("act", [P, UC, N])
            e_ = t1("e_", [P, IC, N])
            em = t1("em", [P, IC, N])
            ln = t1("ln", [P, IC, N])
            delta = t1("delta", [P, IC, N])
            cr = t1("cr", [P, IC, N])
            bx = t1("bx", [P, IC, N])
            H = t1("H", [P, IC, N])
            yb = t1("yb", [P, IC, N])

        q_T, q_Q, q_F, q_S, q4, q5, q6, q7 = bank

        q4b = q4

        def gbank(c):
            return (q7, q5)[c % 2]

        def seqs(ap):
            return ap.rearrange("p (s t) -> p s t", s=SEQ)

        @block.sync
        def _(sp):
            sp.dma_start(xs_of(0), x_d[0]).then_inc(sem["x_loaded"], 16)
            for dst, src in loads:
                sp.dma_start(dst, src, allow_slow_non_contiguous=dst.shape[1] == IC).then_inc(sem["w_loaded"], 16)
            with sp.Fori(1, G) as n:
                sp.wait_ge(sem["x_loaded"], n * 16)
                sp.dma_start(xs_of(n), x_d[bass.ds(n, 1)].rearrange("g p f -> (g p) f")).then_inc(sem["x_loaded"], 16)
            with sp.Fori(0, G) as n:
                sp.wait_ge(sem["b_out"], n + 1)
                sp.dma_start(out_d[bass.ds(n, 1)].rearrange("g p f -> (g p) f"), xs_of(n)).then_inc(sem["stored"], 16)
            sp.wait_ge(sem["stored"], 16 * G)

        @block.gpsimd
        def _(pool):
            nc.gpsimd.memset(ident[:, :], 0.0).then_inc(sem["const_ready"], 1)
            nc.gpsimd.memset(sel[:, :, :], 0.0).then_inc(sem["const_ready"], 1)
            nc.gpsimd.memset(neghalf[:, :], -0.5).then_inc(sem["const_ready"], 1)
            nc.gpsimd.memset(epsc[:, :], EPS).then_inc(sem["const_ready"], 1)
            nc.gpsimd.memset(ones[:, :], 1.0).then_inc(sem["const_ready"], 1)
            nc.gpsimd.memset(a_[:, :, 0:1], 0.0).then_inc(sem["const_ready"], 1)
            nc.gpsimd.memset(Pk[:, :, 0:1], 0.0).then_inc(sem["const_ready"], 1)
            nc.gpsimd.memset(Pv[:, :, 0:1], 0.0).then_inc(sem["const_ready"], 1)
            nc.gpsimd.memset(xi[:, :, :, 0:TAPS - 1], 0.0).then_inc(sem["const_ready"], 1)
            nc.gpsimd.memset(pe_[:, :, NR:], -1.0).then_inc(sem["const_ready"], 1)
            pool.wait_ge(sem["const_ready"], 1)
            nc.gpsimd.affine_select(out=ident[:, :], in_=ident[:, :], compare_op=ALU.not_equal, fill=1.0, base=0,
                                    pattern=[[-1, P]], channel_multiplier=1).then_inc(sem["ident_ready"], 1)
            pool.wait_ge(sem["ident_ready"], 1)
            nc.gpsimd.tensor_copy(identb[:, :], ident[:, :]).then_inc(sem["ident_ready"], 1)
            for b in range(3):
                pool.wait_ge(sem["const_ready"], 2)
                after(pool, sem["sel_ready"], b)
                v = sel[:, :, :].rearrange("k c (h e) -> k c h e", e=E)
                nc.gpsimd.affine_select(out=v, in_=v, compare_op=ALU.not_equal, fill=1.0, base=-NR * b,
                                        pattern=[[-(P // E), RC], [-1, P // E], [0, E]],
                                        channel_multiplier=1).then_inc(sem["sel_ready"], 1)

            def normalise(n, stat, rstd0, rstd_s, centred, xn_s, turned):
                pool.wait_ge(stat, n + 1)
                nc.gpsimd.tensor_tensor(ve[:, :], mv[:, :, 1], epsc[:, :], ALU.add).then_inc(rstd0, 1)
                pool.wait_ge(rstd0, n + 1)
                nc.gpsimd.tensor_tensor(rstd[:, :], ve[:, :], neghalf[:, :], ALU.pow).then_inc(rstd_s, 1)
                pool.wait_ge(rstd_s, n + 1)
                after(pool, turned, n)
                rows = xs_of(n).rearrange("p (j c) -> p j c", j=J)
                mean = mv[:, :, 0:1].to_broadcast([P, J, P])
                nc.gpsimd.tensor_tensor(xn[:, :, :], rows, mean, ALU.subtract).then_inc(centred, 1)
                pool.wait_ge(centred, n + 1)
                nc.gpsimd.tensor_tensor(xn[:, :, :], xn[:, :, :], rstd[:, :].unsqueeze(2).to_broadcast([P, J, P]),
                                        ALU.mult).then_inc(xn_s, 1)

            pool.wait_ge(sem["const_ready"], 4)

            def layer0(n):
                normalise(n, sem["a_stat"], sem["a_rstd0"], sem["a_rstd"], sem["a_centred"], sem["a_xn"], sem["a_xnT"])
                pool.wait_ge(sem["a_wkc"], n + 1)
                pool.wait_ge(sem["a_scanK"], n + 1)
                after(pool, sem["a_rec"], n)
                nc.gpsimd.tensor_tensor(seqs(wk[:, :]), seqs(wkc[:, :]), Pk[:, :, 0:T], ALU.add).then_inc(sem["a_wk"], 1)

            groups(pool, layer0)

            def layer1(n):
                normalise(n, sem["b_stat"], sem["b_rstd0"], sem["b_rstd"], sem["b_centred"], sem["b_xn"], sem["b_xnT"])
                for k in range(IC):
                    pool.wait_ge(sem["b_cr"], IC * n + k + 1)
                    pool.wait_ge(sem["b_scan"], IC * n + k + 1)
                    after(pool, sem["b_s"], n)
                    nc.gpsimd.tensor_tensor(yb[:, k, :], H[:, k, :], cr[:, k, :], ALU.mult).then_inc(sem["b_y"], 1)

            groups(pool, layer1)

        @block.scalar
        def _(actv):
            act_e = nc.scalar
            actv.wait_ge(sem["w_loaded"], W_ALL)
            act_e.activation(sg_[:, :], scal[:, 0:2], ACT.Sign).then_inc(sem["sign_ready"], 1)
            act_e.activation(tch[:, 0:1], chan[:, 0:1], ACT.Exp).then_inc(sem["act_w_ready"], 1)
            actv.wait_ge(sem["act_w_ready"], 1)
            act_e.activation(tch[:, 1:2], tch[:, 0:1], ACT.Exp, scale=-1.0).then_inc(sem["act_w_ready"], 1)
            act_e.activation(tch[:, 2:3], chan[:, 1:2], ACT.Exp).then_inc(sem["act_w_ready"], 1)
            for i, (src, dst, k) in enumerate(turns):
                if i % 2:
                    actv.wait_ge(sem["tr_done"], i + 1)
                    m = dst.shape[0]
                    act_e.copy(dst, bank[i % TB][0:m, 0:dst.shape[1]]).then_inc(sem["act_w_ready"], 1)
            ACT_W = 3 + len(turns) // 2

            def layer0(n):
                actv.wait_ge(sem["a_xnT"], n + 1)
                after(actv, sem["a_xm"], n)
                act_e.activation(a_[:, :, 1:T], seqs(b_T[:, :])[:, :, 0:T - 1], ACT.Copy,
                                 scale=tch[:, 3:4]).then_inc(sem["a_xs"], 1)
                after(actv, sem["a_z"], 8 * n - 4)
                act_e.activation(xh[:, :], b_T[:, :], ACT.Copy, scale=XS).then_inc(sem["a_xh"], 1)
                if not isinstance(n, int):
                    gate(n - 1)
                actv.wait_ge(sem["a_k"], n + 1)
                after(actv, sem["a_ekm"], n)
                act_e.activation(ek[:, :], b_K[:, :], ACT.Exp).then_inc(sem["a_ek"], 1)
                actv.wait_ge(sem["a_r"], n + 1)
                after(actv, sem["a_y2"], n)
                act_e.activation(thr[:, :], b_RX[:, :], ACT.Tanh, scale=0.5).then_inc(sem["a_thr"], 1)
                for q in range(2 * FC):
                    if q == FC:
                        actv.wait_ge(sem["a_ekm"], n + 1)
                        after(actv, sem["a_wk"], n)
                        act_e.activation(wkc[:, :], ekm[:, :], ACT.Copy, scale=tch[:, 2:3],
                                         bias=WK_EPS).then_inc(sem["a_wkc"], 1)
                    actv.wait_ge(sem["a_z"], 8 * n + q + 1)
                    after(actv, sem["a_z"] if q < FC else sem["a_f"], 8 * n if q < FC else n)
                    act_e.activation(hh[:, q // FC, q % FC, :], bank[4 + q % 2][:, :], ACT.Relu).then_inc(sem["a_hi"], 1)

            def gate(n):
                actv.wait_ge(sem["a_f"], n + 1)
                after(actv, sem["a_gp"], n)
                act_e.activation(thf[:, :], b_F[:, :], ACT.Tanh, scale=c3[:, 2:3]).then_inc(sem["a_thf"], 1)

            actv.wait_ge(sem["scal_done"], 1)
            groups(actv, layer0, lambda n: gate(n - 1))

            GELU_SET, EXP_SET = "gelu_and_others", "natural_log_exp_and_others"

            def gate1(n):
                actv.wait_ge(sem["b_down"], n + 1)
                after(actv, sem["b_gp"], n)
                act_e.activation(thf1[:, :], q_F[:, :], ACT.Tanh, scale=0.5).then_inc(sem["b_thf"], 1)

            def layer1(n):
                act_e.preload_act_table_set(GELU_SET)
                actv.wait_ge(sem["b_xnT"], n + 1)
                after(actv, sem["b_up"], UC * n)
                act_e.copy(xc[:, :], q_T[:, :]).then_inc(sem["b_xc"], 1)
                if not isinstance(n, int):
                    gate1(n - 1)
                for k in range(IC):
                    ps = (q4, q5)[k]
                    actv.wait_ge(sem["b_xin"], IC * n + k + 1)
                    after(actv, sem["b_conv"], IC * n * (TAPS - 1))
                    after(actv, sem["b_xc2"], IC * n)
                    act_e.copy(xi[:, k, :, TAPS - 1:], seqs(ps[:, :])).then_inc(sem["b_xi"], 1)
                    act_e.activation(u[:, k, :], ps[:, :], ACT.Identity, scale=cw[:, k, TAPS - 1:TAPS],
                                     bias=cb[:, k:k + 1]).then_inc(sem["b_u0"], 1)
                for k in range(IC):
                    actv.wait_ge(sem["b_res"], IC * n + k + 1)
                    after(actv, sem["b_r2"], IC * n)
                    act_e.activation(th2[:, k, :], (q6, q7)[k][:, :], ACT.Tanh, scale=0.5).then_inc(sem["b_thr"], 1)

                def up(c):
                    actv.wait_ge(sem["b_up"], UC * n + c + 1)
                    after(actv, sem["b_down"], n)
                    act_e.activation(act[:, c, :], (q4, q5)[c % 2][:, :], ACT.Gelu).then_inc(sem["b_act"], 1)

                for c in range(UC):
                    up(c)
                    if c in (2, 5):
                        k = (c - 2) // 3
                        actv.wait_ge(sem["b_conv"], (IC * n + k + 1) * (TAPS - 1))
                        act_e.activation(thu[:, k, :], u[:, k, :], ACT.Tanh, scale=0.5).then_inc(sem["b_thu"], 1)
                act_e.preload_act_table_set(EXP_SET)
                actv.wait_ge(sem["b_lg"], n + 1)
                after(actv, sem["b_gt"], n)
                act_e.activation(pe_[:, :, 0:NR], lg[:, :, :], ACT.Exp).then_inc(sem["b_pe"], 1)
                for k in range(IC):
                    actv.wait_ge(sem["b_d"], IC * n + k + 1)
                    after(actv, sem["b_em"], IC * n)
                    act_e.activation(e_[:, k, :], (q4, q6)[k][:, :], ACT.Exp, bias=bdt[:, k:k + 1]).then_inc(sem["b_e"], 1)
                for k in range(IC):
                    actv.wait_ge(sem["b_em"], IC * n + k + 1)
                    after(actv, sem["b_delta"], IC * n)
                    act_e.activation(ln[:, k, :], em[:, k, :], ACT.Ln, bias=1.0).then_inc(sem["b_ln"], 1)
                actv.wait_ge(sem["b_gtT"], n + 1)
                after(actv, sem["b_gate"], RC * n)
                act_e.copy(gT[:, :].rearrange("r (p j) -> r j p", j=J),
                           q_Q[0:3 * NR, 0:N // 2].bitcast(BF16).rearrange("r (j p) -> r j p", j=J)).then_inc(sem["b_gT"], 1)

            def tail1(n):
                act_e.preload_act_table_set(GELU_SET)
                gate1(n - 1)

            groups(actv, layer1, tail1)

        @block.vector
        def _(dve):
            v = nc.vector
            dve.wait_ge(sem["w_loaded"], W_ALL)
            dve.wait_ge(sem["const_ready"], 10)
            dve.wait_ge(sem["sign_ready"], 1)
            dve.wait_ge(sem["act_w_ready"], 3)
            steps = [0]

            def link(ins):
                steps[0] += 1
                ins.then_inc(sem["scal_ready"], 1)
                dve.wait_ge(sem["scal_ready"], steps[0])

            link(v.tensor_scalar(w0c[:, :], sg_[:, 0:1], 2.0 * W0S, None, ALU.mult))
            link(v.tensor_tensor(w0d[:, :], k0_u[:, 0, :], k0_u[:, 1, :], ALU.subtract))
            link(v.tensor_scalar(w0[:, :], w0d[:, :], w0c[:, 0:1], None, ALU.mult))
            link(v.tensor_scalar(w1c[:, 0:1], sg_[:, 1:2], 2.0 * W1S, None, ALU.mult))
            link(v.tensor_scalar(w1c[:, 1:2], sg_[:, 1:2], -W1S, None, ALU.mult))
            link(v.tensor_scalar(w1[:, :, :], k1_u[:, :, :], w1c[:, 0:1], w1c[:, 1:2], ALU.mult, ALU.add))
            link(v.tensor_scalar(w2[:, :, :], k2_u[:, :, :], 2.0, -1.0, ALU.mult, ALU.add))
            link(v.tensor_tensor(sab[:, :], scal[:, 0:2], sg_[:, :], ALU.mult))
            link(v.tensor_tensor(c3[:, 0:1], sab[:, 0:1], sab[:, 1:2], ALU.mult))
            link(v.scalar_tensor_tensor(c3[:, 1:2], c3[:, 0:1], FS, scal[:, 2:3], ALU.mult, ALU.mult))
            link(v.tensor_scalar(c3[:, 2:3], c3[:, 1:2], 0.5, None, ALU.mult))
            link(v.tensor_scalar(c3[:, 3:4], c3[:, 1:2], 0.25, None, ALU.mult))
            link(v.tensor_scalar(tch[:, 3:4], chan[:, 2:3], -1.0, 1.0, ALU.mult, ALU.add))
            link(v.tensor_scalar(dec[:, 0:P], ones[:, :], tch[:, 1:2], None, ALU.mult))
            link(v.tensor_scalar(dec[:, P:2 * P], ones[:, :], tch[:, 1:2], None, ALU.mult))
            link(v.tensor_scalar(wc[:, :, :], wx[:, :, 2 * DS:], 0.5, None, ALU.mult))
            link(v.tensor_reduce(wbs[:, :], wx[:, :, DS:2 * DS], AX.X, ALU.add))
            for k in range(IC):
                link(v.tensor_scalar(wb[:, k, :], ones[:, :], wbs[:, k:k + 1], 0.25, ALU.mult, ALU.mult))
            v.tensor_scalar(c3[:, 0:1], c3[:, 1:2], 1.0, None, ALU.mult).then_inc(sem["scal_done"], 1)
            for i, (src, dst, k) in enumerate(turns):
                if i % 2 == 0:
                    dve.wait_ge(sem["tr_done"], i + 1)
                    m = dst.shape[0]
                    v.tensor_copy(dst, bank[i % TB][0:m, 0:dst.shape[1]]).then_inc(sem["w_ready"], 1)
            for k in range(IC):
                dve.wait_ge(sem["wdt_done"], k + 1)
                v.tensor_scalar(wdel[:, k, :], bank[4 + k][:, 0:DI], 0.5, None, ALU.mult).then_inc(sem["wt_ready"], 1)

            def row_stats(n, xn_sem, loaded):
                if loaded:
                    dve.wait_ge(sem["x_loaded"], n * 16 + 16)
                for j in range(J):
                    last = v.bn_stats(st[:, j, :], x_all[:, bass.ds(n * N + j * P, P)])
                last.then_inc(sem["bn_done"], 1)

            def row_moments(n, out_sem):
                for j in range(J):
                    last = v.bn_aggr(mv[:, j, :], st[:, j, :])
                last.then_inc(out_sem, 1)

            def low(n, q):
                dve.wait_ge(sem["a_hi"], 8 * n + q + 1)
                after(dve, sem["a_z"] if q < FC else sem["a_f"], 8 * n if q < FC else n)
                v.scalar_tensor_tensor(hl[:, q // FC, q % FC, :], bank[4 + q % 2][:, :], 0.0,
                                       hh[:, q // FC, q % FC, :], ALU.max, ALU.subtract).then_inc(sem["a_lo"], 1)

            def final_product(n):
                dve.wait_ge(sem["a_thf"], n + 1)
                after(dve, sem["a_sg"], n)
                v.scalar_tensor_tensor(gp[:, :], thf[:, :], 1.0, b_F[:, :], ALU.add, ALU.mult).then_inc(sem["a_gp"], 1)
                dve.wait_ge(sem["a_gp"], n + 1)
                dve.wait_ge(sem["a_s"], n + 1)
                after(dve, sem["a_sgT"], n)
                v.scalar_tensor_tensor(sg[:, :], b_S[:, :], c3[:, 3:4], gp[:, :], ALU.mult, ALU.mult).then_inc(sem["a_sg"], 1)

            def final_sum(n):
                dve.wait_ge(sem["a_sgT"], n + 1)
                v.tensor_tensor(xs_of(n), xs_of(n), b_RX[:, :], ALU.add).then_inc(sem["a_x1"], 1)

            def layer0(n, ahead=True):
                first = isinstance(n, int) and n == 0
                dve.wait_ge(sem["a_xh"], n + 1)
                after(dve, sem["a_r"], n)
                v.scalar_tensor_tensor(xm[:, :], b_T[:, :], chan[:, 2:3], a_[:, :, :].rearrange("p s t -> p (s t)"),
                                       ALU.mult, ALU.add).then_inc(sem["a_xm"], 1)
                after(dve, sem["a_z"], 8 * n - 4)
                v.scalar_tensor_tensor(xl[:, :], b_T[:, :], XS, xh[:, :], ALU.mult, ALU.subtract).then_inc(sem["a_xl"], 1)
                dve.wait_ge(sem["a_ek"], n + 1)
                after(dve, sem["a_wkc"], n)
                v.tensor_scalar(ekm[:, :], ek[:, :], math.exp(K_CAP), None, ALU.min).then_inc(sem["a_ekm"], 1)
                dve.wait_ge(sem["a_ekm"], n + 1)
                dve.wait_ge(sem["a_v"], n + 1)
                v.tensor_tensor(kv[:, :], ekm[:, :], b_V[:, :], ALU.mult).then_inc(sem["a_kv"], 1)
                for q in range(FC):
                    low(n, q)
                after(dve, sem["a_wk"], n)
                for s in range(SEQ):
                    last = v.tensor_tensor_scan(Pk[:, s, 1:], dec[:, :], ekm[:, s * T:(s + 1) * T], 0.0, ALU.mult, ALU.add)
                last.then_inc(sem["a_scanK"], 1)
                dve.wait_ge(sem["a_kv"], n + 1)
                for s in range(SEQ):
                    last = v.tensor_tensor_scan(Pv[:, s, 1:], dec[:, :], kv[:, s * T:(s + 1) * T], 0.0, ALU.mult, ALU.add)
                last.then_inc(sem["a_scanV"], 1)
                if not first:
                    final_product(n - 1)
                low(n, FC)
                dve.wait_ge(sem["a_scanV"], n + 1)
                v.scalar_tensor_tensor(seqs(wkv[:, :]), seqs(kv[:, :]), tch[:, 2:3], Pv[:, :, 0:T],
                                       ALU.mult, ALU.add).then_inc(sem["a_wkv"], 1)
                if ahead:
                    row_stats(n + 1, sem["a_xn"], True)
                    dve.wait_ge(sem["a_xn"], n + 1)
                    dve.wait_ge(sem["bn_done"], n + 2)
                dve.wait_ge(sem["a_wk"], n + 1)
                v.reciprocal(rec[:, 0:N // 2], wk[:, 0:N // 2])
                if ahead:
                    row_moments(n + 1, sem["a_stat"])
                low(n, FC + 1)
                v.reciprocal(rec[:, N // 2:], wk[:, N // 2:]).then_inc(sem["a_rec"], 1)
                low(n, FC + 2)
                dve.wait_ge(sem["a_rec"], n + 1)
                v.tensor_tensor(yq[:, :], wkv[:, :], rec[:, :], ALU.mult).then_inc(sem["a_y"], 1)
                low(n, FC + 3)
                dve.wait_ge(sem["a_y"], n + 1)
                dve.wait_ge(sem["a_thr"], n + 1)
                after(dve, sem["a_s"], n)
                v.scalar_tensor_tensor(y2[:, :], thr[:, :], 1.0, yq[:, :], ALU.add, ALU.mult).then_inc(sem["a_y2"], 1)
                if not first:
                    final_sum(n - 1)

            row_stats(0, sem["a_xn"], True)
            dve.wait_ge(sem["bn_done"], 1)
            row_moments(0, sem["a_stat"])
            layer0(0)
            with dve.Fori(1, G - 1) as n:
                layer0(n)
            layer0(G - 1, ahead=False)
            final_product(G - 1)
            final_sum(G - 1)

            def top_gates(n):
                dve.wait_ge(sem["b_pe"], n + 1)
                v.reduce_sum(sm[:, :], pe_[:, :, 0:NR], AX.X).then_inc(sem["b_sum"], 1)
                for j in range(J):
                    last = v.max(top[:, j, :], pe_[:, j, 0:NR])
                last.then_inc(sem["b_top"], 1)
                dve.wait_ge(sem["b_top"], n + 1)
                v.memset(top[:, :, TOP_K:], -1.0).then_inc(sem["b_top2"], 1)
                dve.wait_ge(sem["b_sum"], n + 1)
                dve.wait_ge(sem["b_top2"], n + 1)
                v.reciprocal(rs[:, :], sm[:, :]).then_inc(sem["b_rs"], 1)
                for j in range(J):
                    last = v.match_replace(rep[:, j, :], top[:, j, :], pe_[:, j, :], 0.0)
                last.then_inc(sem["b_rep"], 1)
                dve.wait_ge(sem["b_rep"], n + 1)
                v.tensor_tensor(gt[:, :, :], pe_[:, :, 0:NR], rep[:, :, 0:NR], ALU.subtract).then_inc(sem["b_gt"], 1)
                dve.wait_ge(sem["b_gt"], n + 1)
                dve.wait_ge(sem["b_rs"], n + 1)
                v.tensor_tensor(gn[:, :, :], gt[:, :, :], rs[:, :].unsqueeze(2).to_broadcast([P, J, NR]),
                                ALU.mult).then_inc(sem["b_gn"], 1)
                dve.wait_ge(sem["b_gn"], n + 1)
                after(dve, sem["b_gtT"], n)
                v.tensor_copy(g3[:, :, 0, :], gn[:, :, :]).then_inc(sem["b_g1"], 1)
                dve.wait_ge(sem["b_g1"], n + 1)
                v.tensor_tensor(gr1[:, :, :], gn[:, :, :], g3[:, :, 0, :], ALU.subtract).then_inc(sem["b_g2"], 1)
                dve.wait_ge(sem["b_g2"], n + 1)
                v.tensor_copy(g3[:, :, 1, :], gr1[:, :, :]).then_inc(sem["b_g3"], 1)
                dve.wait_ge(sem["b_g3"], n + 1)
                v.tensor_tensor(g3[:, :, 2, :], gr1[:, :, :], g3[:, :, 1, :], ALU.subtract).then_inc(sem["b_g5"], 1)

            def final_product1(n):
                dve.wait_ge(sem["b_thf"], n + 1)
                after(dve, sem["b_sg"], n)
                v.scalar_tensor_tensor(gp1[:, :], thf1[:, :], 1.0, q_F[:, :], ALU.add, ALU.mult).then_inc(sem["b_gp"], 1)
                dve.wait_ge(sem["b_gp"], n + 1)
                dve.wait_ge(sem["b_s"], n + 1)
                after(dve, sem["b_sgT"], n)
                v.scalar_tensor_tensor(sg1[:, :], q_S[:, :], 0.25, gp1[:, :], ALU.mult, ALU.mult).then_inc(sem["b_sg"], 1)

            def final_sum1(n):
                dve.wait_ge(sem["b_sgT"], n + 1)
                v.tensor_tensor(xs_of(n), xs_of(n), q_Q[:, :], ALU.add).then_inc(sem["b_out"], 1)

            def layer1(n, ahead=True):
                first = isinstance(n, int) and n == 0
                for k in range(IC):
                    for t in range(TAPS - 1):
                        i = (IC * n + k) * (TAPS - 1) + t
                        if t == 0:
                            dve.wait_ge(sem["b_u0"], IC * n + k + 1)
                        else:
                            dve.wait_ge(sem["b_conv"], i)
                        uk = seqs(u[:, k, :])
                        v.scalar_tensor_tensor(uk, xi[:, k, :, t:t + T], cw[:, k, t:t + 1], uk,
                                               ALU.mult, ALU.add).then_inc(sem["b_conv"], 1)
                if not first:
                    final_product1(n - 1)
                for k in range(IC):
                    dve.wait_ge(sem["b_thu"], IC * n + k + 1)
                    after(dve, sem["b_b"], n)
                    v.scalar_tensor_tensor(xc2[:, k, :], thu[:, k, :], 1.0, u[:, k, :], ALU.add,
                                           ALU.mult).then_inc(sem["b_xc2"], 1)
                for k in range(IC):
                    dve.wait_ge(sem["b_thr"], IC * n + k + 1)
                    v.scalar_tensor_tensor(r2[:, k, :], th2[:, k, :], 1.0, (q6, q7)[k][:, :], ALU.add,
                                           ALU.mult).then_inc(sem["b_r2"], 1)
                dve.wait_ge(sem["b_rout"], n + 1)
                lp = q_Q[:, 0:J * NR].rearrange("p (j r) -> p j r", r=NR)
                v.tensor_reduce(mx[:, :], lp, AX.X, ALU.max).then_inc(sem["b_mx"], 1)
                dve.wait_ge(sem["b_mx"], n + 1)
                v.tensor_tensor(lg[:, :, :], lp, mx[:, :].unsqueeze(2).to_broadcast([P, J, NR]),
                                ALU.subtract).then_inc(sem["b_lg"], 1)
                if not first:
                    final_sum1(n - 1)
                top_gates(n)
                for k in range(IC):
                    dve.wait_ge(sem["b_e"], IC * n + k + 1)
                    v.tensor_scalar(em[:, k, :], e_[:, k, :], math.exp(SP_CAP), None, ALU.min).then_inc(sem["b_em"], 1)
                for k in range(IC):
                    dve.wait_ge(sem["b_ln"], IC * n + k + 1)
                    v.scalar_tensor_tensor(delta[:, k, :], (q4, q6)[k][:, :], bdt[:, k:k + 1], ln[:, k, :],
                                           ALU.add, ALU.max).then_inc(sem["b_delta"], 1)
                for k in range(IC):
                    dve.wait_ge(sem["b_c"], IC * n + k + 1)
                    after(dve, sem["b_y"], IC * n)
                    v.tensor_tensor(cr[:, k, :], (q7, q5)[k][:, :], r2[:, k, :], ALU.mult).then_inc(sem["b_cr"], 1)
                if ahead:
                    row_stats(n + 1, sem["b_xn"], False)
                    dve.wait_ge(sem["b_xn"], n + 1)
                    dve.wait_ge(sem["bn_done"], G + n + 2)
                dve.wait_ge(sem["b_b"], n + 1)
                for k in range(IC):
                    v.tensor_tensor(bx[:, k, :], xc2[:, k, :], q4b[:, :], ALU.mult).then_inc(sem["b_bx"], 1)
                if ahead:
                    row_moments(n + 1, sem["b_stat"])
                for c in range(RC):
                    gated(n, c)
                    if c in (1, 3):
                        k = c // 2
                        dve.wait_ge(sem["b_bx"], IC * n + k + 1)
                        dve.wait_ge(sem["b_delta"], IC * n + k + 1)
                        after(dve, sem["b_y"], IC * n)
                        for s in range(SEQ):
                            w = slice(s * T, (s + 1) * T)
                            last = v.tensor_tensor_scan(H[:, k, w], delta[:, k, w], bx[:, k, w], 0.0, ALU.mult, ALU.add)
                        last.then_inc(sem["b_scan"], 1)

            def gated(n, c):
                dve.wait_ge(sem["b_gate"], RC * n + c + 1)
                v.tensor_tensor(act[:, c + 1, :], act[:, c + 1, :], gbank(c)[:, :], ALU.mult).then_inc(sem["b_actg"], 1)

            dve.wait_ge(sem["a_x1"], G)
            dve.wait_ge(sem["a_xn"], G)
            row_stats(0, sem["b_xn"], False)
            dve.wait_ge(sem["bn_done"], G + 1)
            row_moments(0, sem["b_stat"])
            layer1(0)
            with dve.Fori(1, G - 1) as n:
                layer1(n)
            layer1(G - 1, ahead=False)
            final_product1(G - 1)
            final_sum1(G - 1)

        @block.tensor
        def _(pe):
            def mm(ps, lhsT, rhs, start, stop):
                return nc.tensor.matmul(ps, lhsT, rhs, start=start, stop=stop)

            pe.wait_ge(sem["w_loaded"], W_ALL)
            pe.wait_ge(sem["ident_ready"], 2)
            for i, (src, dst, k) in enumerate(turns):
                if i >= TB:
                    pe.wait_ge(sem["act_w_ready"] if i % 2 else sem["w_ready"], 3 + (i - TB) // 2 + 1 if i % 2 else (i - TB) // 2 + 1)
                rows = src.shape[0]
                cols = src.shape[1]
                nc.tensor.transpose(bank[i % TB][0:cols, 0:rows], src, ident[0:rows, 0:rows]).then_inc(sem["tr_done"], 1)
            pe.wait_ge(sem["w_ready"], (len(turns) + 1) // 2)
            pe.wait_ge(sem["act_w_ready"], 3 + len(turns) // 2)
            for k in range(IC):
                mm(bank[4 + k][:, 0:DI], wxsT[:, k, :], wdt[:, :], True, True).then_inc(sem["wdt_done"], 1)
            pe.wait_ge(sem["scal_done"], 1)
            pe.wait_ge(sem["wt_ready"], IC)

            def attention_out(n):
                pe.wait_ge(sem["a_y2"], n + 1)
                after(pe, sem["a_sg"], n)
                mm(b_S[:, :], wsqT[:, 3, :], y2[:, :], True, True).then_inc(sem["a_s"], 1)

            def turn_back(n):
                pe.wait_ge(sem["a_sg"], n + 1)
                pe.wait_ge(sem["a_thr"], n + 2 if not isinstance(n, int) else n + 1)
                for j in range(J):
                    last = nc.tensor.transpose(b_RX[:, j * P:(j + 1) * P], sg[:, j::J], ident[:, :])
                last.then_inc(sem["a_sgT"], 1)

            def layer0(n):
                first = isinstance(n, int) and n == 0
                pe.wait_ge(sem["a_xn"], n + 1)
                after(pe, sem["a_xl"], n)
                for j in range(J):
                    last = nc.tensor.transpose(b_T[:, j::J], xn[:, j, :], ident[:, :])
                last.then_inc(sem["a_xnT"], 1)
                pe.wait_ge(sem["a_xm"], n + 1)
                after(pe, sem["a_ek"], n)
                mm(b_K[:, :], wsqT[:, 0, :], xm[:, :], True, True).then_inc(sem["a_k"], 1)
                after(pe, sem["a_kv"], n)
                mm(b_V[:, :], wsqT[:, 1, :], xm[:, :], True, True).then_inc(sem["a_v"], 1)
                mm(b_RX[:, :], wsqT[:, 2, :], xm[:, :], True, True).then_inc(sem["a_r"], 1)
                pe.wait_ge(sem["a_xl"], n + 1)
                for m in range(FC):
                    after(pe, sem["a_lo"], 8 * n + m - 1)
                    mm(bank[4 + m % 2][:, :], w0[:, m * P:(m + 1) * P], xh[:, :], True, False)
                    mm(bank[4 + m % 2][:, :], w0[:, m * P:(m + 1) * P], xl[:, :], False, True).then_inc(sem["a_z"], 1)
                if not first:
                    attention_out(n - 1)
                for m in range(FC):
                    for k in range(FC):
                        pe.wait_ge(sem["a_lo"], 8 * n + max(k + 1, FC + m - 1))
                        w = w1[:, k, m * P:(m + 1) * P]
                        mm(bank[4 + m % 2][:, :], w, hh[:, 0, k, :], k == 0, False)
                        last = mm(bank[4 + m % 2][:, :], w, hl[:, 0, k, :], False, k == FC - 1)
                    last.then_inc(sem["a_z"], 1)
                after(pe, sem["a_gp"], n)
                for k in range(FC):
                    pe.wait_ge(sem["a_lo"], 8 * n + FC + k + 1)
                    mm(b_F[:, :], w2[:, k, :], hh[:, 1, k, :], k == 0, False)
                    last = mm(b_F[:, :], w2[:, k, :], hl[:, 1, k, :], False, k == FC - 1)
                last.then_inc(sem["a_f"], 1)
                if not first:
                    turn_back(n - 1)

            def tail0(n):
                attention_out(n - 1)
                turn_back(n - 1)

            groups(pe, layer0, tail0)

            def state_out(n):
                pe.wait_ge(sem["b_y"], IC * n + IC)
                after(pe, sem["b_sg"], n)
                for k in range(IC):
                    last = mm(q_S[:, :], w_out[:, k, :], yb[:, k, :], k == 0, k == IC - 1)
                last.then_inc(sem["b_s"], 1)

            def turn_back1(n):
                pe.wait_ge(sem["b_sg"], n + 1)
                pe.wait_ge(sem["b_lg"], n + 2 if not isinstance(n, int) else n + 1)
                for j in range(J):
                    last = nc.tensor.transpose(q_Q[:, j * P:(j + 1) * P], sg1[:, j::J], ident[:, :])
                last.then_inc(sem["b_sgT"], 1)

            def layer1(n):
                first = isinstance(n, int) and n == 0
                pe.wait_ge(sem["b_xn"], n + 1)
                after(pe, sem["b_xc"], n)
                if first:
                    pe.wait_ge(sem["a_x1"], G)
                for j in range(J):
                    last = nc.tensor.transpose(q_T[:, j::J], xn[:, j, :], ident[:, :])
                last.then_inc(sem["b_xnT"], 1)
                pe.wait_ge(sem["b_xc"], n + 1)
                after(pe, sem["b_bx"], IC * n)
                after(pe, sem["b_actg"], RC * n)
                after(pe, sem["b_delta"], IC * n)
                for k in range(IC):
                    mm((q4, q5)[k][:, :], w_in[:, k * P:(k + 1) * P], xc[:, :], True, True).then_inc(sem["b_xin"], 1)
                for k in range(IC):
                    mm((q6, q7)[k][:, :], w_in[:, DI + k * P:DI + (k + 1) * P], xc[:, :], True, True).then_inc(sem["b_res"], 1)
                after(pe, sem["b_gT"], n)
                for j in range(J):
                    last = mm(q_Q[:, j * NR:(j + 1) * NR], xc[:, j::J], rwT[:, :], True, True)
                last.then_inc(sem["b_rout"], 1)
                if not first:
                    state_out(n - 1)
                for c in range(UC):
                    if c < 2:
                        pe.wait_ge(sem["b_u0"], IC * n + c + 1)
                    else:
                        pe.wait_ge(sem["b_act"], UC * n + c - 1)
                    mm((q4, q5)[c % 2][:, :], upT[:, c, :], xc[:, :], True, True).then_inc(sem["b_up"], 1)
                    if c == 5 and not first:
                        turn_back1(n - 1)
                pe.wait_ge(sem["b_xc2"], IC * n + IC)
                pe.wait_ge(sem["b_act"], UC * n + UC)
                pe.wait_ge(sem["b_r2"], IC * n + IC)
                for m in range(IC):
                    for k in range(IC):
                        last = mm((q4, q6)[m][:, :], wdel[:, k, m * P:(m + 1) * P], xc2[:, k, :], k == 0, k == IC - 1)
                    last.then_inc(sem["b_d"], 1)
                for m in range(IC):
                    for k in range(IC):
                        last = mm((q7, q5)[m][:, :], wc[:, k, m * P:(m + 1) * P], xc2[:, k, :], k == 0, k == IC - 1)
                    last.then_inc(sem["b_c"], 1)
                pe.wait_ge(sem["b_delta"], IC * n + 1)
                for k in range(IC):
                    last = mm(q4b[:, :], wb[:, k, :], xc2[:, k, :], k == 0, k == IC - 1)
                last.then_inc(sem["b_b"], 1)
                pe.wait_ge(sem["b_g5"], n + 1)
                if not first:
                    pe.wait_ge(sem["b_out"], n)
                after(pe, sem["b_gp"], n)
                mm(q_F[:, :], dnT[:, 0, :], act[:, 0, :], True, False)
                gps = q_Q[0:3 * NR, 0:N // 2].bitcast(BF16)
                for j in range(J):
                    last = nc.tensor.transpose(gps[:, j * P:(j + 1) * P], g3[:, j, :, :].rearrange("p a r -> p (a r)"),
                                               identb[:, :])
                last.then_inc(sem["b_gtT"], 1)
                pe.wait_ge(sem["b_gT"], n + 1)

                def spread(c):
                    if c < 2:
                        pe.wait_ge(sem["b_cr"], IC * n + c + 1)
                    else:
                        pe.wait_ge(sem["b_actg"], RC * n + c - 1)
                    mm(gbank(c)[:, :], sel[:, c, :], gT[:, :], True, True).then_inc(sem["b_gate"], 1)

                spread(0)
                spread(1)
                for c in range(RC):
                    pe.wait_ge(sem["b_actg"], RC * n + c + 1)
                    last = mm(q_F[:, :], dnT[:, c + 1, :], act[:, c + 1, :], False, c == RC - 1)
                    if c + 2 < RC:
                        spread(c + 2)
                last.then_inc(sem["b_down"], 1)

            def tail1(n):
                state_out(n - 1)
                turn_back1(n - 1)

            groups(pe, layer1, tail1)


_INS = ["L0_attn_x", "L0_attn_time_decay", "L0_attn_time_first", "L0_attn_time_mix", "L0_attn_Wk", "L0_attn_Wv",
        "L0_attn_Wr", "L0_attn_Wo", "L0_ffn_k0", "L0_ffn_k1", "L0_ffn_k2", "L0_ffn_s0", "L0_ffn_s1", "L0_ffn_s2",
        "L1_attn_W_in", "L1_attn_conv_w", "L1_attn_conv_b", "L1_attn_W_x", "L1_attn_W_dt", "L1_attn_b_dt",
        "L1_attn_W_out", "L1_ffn_shared_up", "L1_ffn_shared_down", "L1_ffn_routed_up", "L1_ffn_routed_down",
        "L1_ffn_router_w"]


def kernel(**inputs):
    import numpy as _np
    import concourse.bacc as _bacc
    from concourse import mybir as _mybir
    from concourse.bass_utils import run_bass_kernel_spmd as _run

    nc = _bacc.Bacc("TRN2", target_bir_lowering=False, num_devices=1)
    arrays, args = {}, {}
    for name in _INS:
        a = _np.ascontiguousarray(inputs[name])
        if a.ndim == 0:
            a = a.reshape(1)
        arrays[f"in_{name}"] = a
        args[name] = nc.dram_tensor(f"in_{name}", a.shape, _mybir.dt.from_np(a.dtype), kind="ExternalInput").ap()
    out = nc.dram_tensor("out_0", inputs["L0_attn_x"].shape, F32, kind="ExternalOutput").ap()
    build(nc, args, out)
    r = _run(nc, [arrays], core_ids=[0])
    return r.results[0]["out_0"]
```

```python
from contextlib import ExitStack
import math

import concourse.bass as bass
from concourse import mybir

ALU = mybir.AluOpType
ACT = mybir.ActivationFunctionType
AX = mybir.AxisListType
F32 = mybir.dt.float32
F16 = mybir.dt.float16
BF16 = mybir.dt.bfloat16
U8 = mybir.dt.uint8

P = 128
EPS = 1e-5
ARENA = 21 * 1024
WK_EPS = 1e-9
K_CAP = 60.0
SP_CAP = 30.0
XS = 2.0 ** 11
W0S = 2.0 ** -4
W1S = 2.0 ** -9
FS = 4.0 * 2.0 ** 2

SEM_NAMES = """
x_loaded wa_loaded wb_loaded ident_ready sel_ready const_ready signs_ready chan_ready chain const_done
square_turned square_ready absmax_ready absmax_all pow2_ready prep_turned prep_high prep_out prep_sbuf
bn_done
a_stat a_vareps a_rstd a_centred a_xn a_xnT a_prev a_xh a_xm a_xl a_k a_v a_r a_ek a_ekm a_kv a_scanK a_scanV
a_wkc a_kvc a_wk a_wkv a_thr a_sr a_ysr a_rec a_y a_z0 a_z1 a_hi0 a_hi1 a_lo0 a_lo1 a_s a_f a_thf a_gp a_sg a_sgT a_x1
b_stat b_vareps b_rstd b_centred b_xn b_xnT b_xh b_xl b_xin b_res b_rout b_u0 b_conv b_thu b_xc2 b_thr b_r2
b_mx b_lg b_pe b_sum b_rs b_top b_fill b_rep b_gt b_gn b_g1 b_g2 b_g3 b_g4 b_gtT b_gT
b_up b_act b_actg b_gate b_down b_d b_e b_em b_ln b_delta b_c b_cr b_b b_bx b_scan b_y b_s b_thf b_gp b_sg b_sgT b_out
stored
""".split()


def build(nc, A, out):
    B, T, C = A["L0_attn_x"].shape
    SEQ = 512 // T
    N = SEQ * T
    J = N // P
    G = B * T // N
    F = A["L0_ffn_k0"].shape[1]
    FC = F // P
    DI = A["L1_attn_W_in"].shape[1] // 2
    IC = DI // P
    DS = A["L1_attn_W_dt"].shape[0]
    TAPS = A["L1_attn_conv_w"].shape[2]
    NR, E, _ = A["L1_ffn_routed_up"].shape
    NS = A["L1_ffn_shared_up"].shape[0]
    TOP_K = 4
    UC = (NS + NR) * E // P
    RC = NR * E // P

    x_d = A["L0_attn_x"].rearrange("b t c -> (b t) c").rearrange("(g p j) c -> g p (j c)", p=P, j=J)
    out_d = out.rearrange("b t c -> (b t) c").rearrange("(g p j) c -> g p (j c)", p=P, j=J)

    with ExitStack() as ctx:
        def sb(name, shape, dt=F32):
            return ctx.enter_context(nc.sbuf_tensor(name, shape, dt))

        sem = {n: ctx.enter_context(nc.semaphore(n)) for n in SEM_NAMES}

        bank = [ctx.enter_context(nc.psum_tensor(f"bank{i}", [P, 512], F32)) for i in range(8)]

        x_all = sb("x_all", [P, G * N])
        ident = sb("ident", [P, P])
        identb = sb("identb", [P, P], BF16)
        ones = sb("ones", [P, P])
        neghalf = sb("neghalf", [P, J])
        epsc = sb("epsc", [P, J])
        sel = sb("sel", [3 * NR, RC, P], BF16)

        wsq = sb("wsq", [P, 4, P])
        k0_u = sb("k0_u", [P, 2, F], U8)
        k1_u = sb("k1_u", [P, FC, F], U8)
        k2_u = sb("k2_u", [P, FC, P], U8)
        scal = sb("scal", [P, 3])
        chan = sb("chan", [P, 3])
        w_in = sb("w_in", [P, 2 * DI])
        cw = sb("cw", [P, IC, TAPS])
        cb = sb("cb", [P, IC])
        bdt = sb("bdt", [P, IC])
        wx = sb("wx", [P, IC, 2 * DS + DI])
        wdt = sb("wdt", [DS, DI])
        w_out = sb("w_out", [P, IC, P])
        up_n = sb("up_n", [P, UC, P])
        dn_n = sb("dn_n", [P, UC, P])
        rw_n = sb("rw_n", [NR, P])

        wsqT = sb("wsqT", [P, 4, P])
        w0 = sb("w0", [P, F], F16)
        w0d = sb("w0d", [P, F])
        w1 = sb("w1", [P, FC, F], F16)
        w2 = sb("w2", [P, FC, P], F16)
        sg_ = sb("sg_", [P, 2])
        sab = sb("sab", [P, 2])
        w0c = sb("w0c", [P, 1])
        w1c = sb("w1c", [P, 2])
        c3 = sb("c3", [P, 4])
        tch = sb("tch", [P, 4])
        dec = sb("dec", [P, T])
        upH = sb("upH", [P, UC * P], F16)
        upL = sb("upL", [P, UC * P], F16)
        rwH = sb("rwH", [P, NR], F16)
        rwL = sb("rwL", [P, NR], F16)
        w_inH = sb("w_inH", [P, 2 * DI], F16)
        w_inL = sb("w_inL", [P, 2 * DI], F16)
        amax = sb("amax", [P, 3])
        pow2 = sb("pow2", [P, 3])
        wsc = sb("wsc", [P, 3])
        inv = sb("inv", [P, 3])
        hinv = sb("hinv", [P, 1])
        cwi = sb("cwi", [P, IC])
        dnT = sb("dnT", [P, UC, P])
        wxsT = sb("wxsT", [DS, IC, P])
        wdel = sb("wdel", [P, IC, DI])
        wc = sb("wc", [P, IC, DI])
        wbs = sb("wbs", [P, IC])
        wb = sb("wb", [P, IC, P])

        st = sb("st", [P, J, 6])
        mv = sb("mv", [P, J, 2])
        ve = sb("ve", [P, J])
        rstd = sb("rstd", [P, J])
        xn = sb("xn", [P, J, P])
        xh = sb("xh", [P, N], F16)
        xl = sb("xl", [P, N], F16)
        thf = sb("thf", [P, N])
        gp = sb("gp", [P, N])
        sg = sb("sg", [P, N])
        prev = sb("prev", [P, SEQ, T])
        Pk = sb("Pk", [P, SEQ, T + 1])
        Pv = sb("Pv", [P, SEQ, T + 1])
        xi = sb("xi", [P, IC, SEQ, T + TAPS - 1])
        pe_ = sb("pe_", [P, J, NR + TOP_K])

        arena = sb("arena", [P, ARENA])
        used = {0: 0, 1: 0}

        def tile(layer, shape, dt=F32):
            size = math.prod(shape[1:]) * (2 if dt in (F16, BF16) else 4) // 4
            flat = arena[0:shape[0], used[layer]:used[layer] + size]
            used[layer] += size
            flat = flat if dt == F32 else flat.bitcast(dt)
            names = "abcd"[:len(shape) - 1]
            if len(names) == 1:
                return flat
            return flat.rearrange(f"p ({' '.join(names)}) -> p {' '.join(names)}", **dict(zip(names, shape[1:])))

        xm = tile(0, [P, N])
        ek = tile(0, [P, N])
        ekm = tile(0, [P, N])
        kv = tile(0, [P, N])
        wkc = tile(0, [P, N])
        kvc = tile(0, [P, N])
        wk = tile(0, [P, N])
        wkv = tile(0, [P, N])
        rec = tile(0, [P, N])
        thr = tile(0, [P, N])
        sr = tile(0, [P, N])
        ysr = tile(0, [P, N])
        ya = tile(0, [P, N])
        hh = tile(0, [P, 2, FC, N], F16)
        hl = tile(0, [P, 2, FC, N], F16)
        u = tile(1, [P, IC, N])
        thu = tile(1, [P, IC, N])
        xc2 = tile(1, [P, IC, N])
        th2 = tile(1, [P, IC, N])
        r2 = tile(1, [P, IC, N])
        lg = tile(1, [P, J, NR])
        mx = tile(1, [P, J])
        sm = tile(1, [P, J])
        rs = tile(1, [P, J])
        top = tile(1, [P, J, 8])
        rep = tile(1, [P, J, NR + TOP_K])
        gt = tile(1, [P, J, NR])
        gn = tile(1, [P, J, NR])
        gr = tile(1, [P, J, NR])
        g3 = tile(1, [P, J, 3, NR], BF16)
        gT = tile(1, [3 * NR, N], BF16)
        act = tile(1, [P, UC, N])
        e_ = tile(1, [P, IC, N])
        em = tile(1, [P, IC, N])
        lnv = tile(1, [P, IC, N])
        delta = tile(1, [P, IC, N])
        cr = tile(1, [P, IC, N])
        bx = tile(1, [P, IC, N])
        H = tile(1, [P, IC, N])
        yb = tile(1, [P, IC, N])

        loads_a = [(wsq[:, i, :], A["L0_attn_" + n]) for i, n in enumerate(("Wk", "Wv", "Wr", "Wo"))]
        loads_a += [
            (chan[:, 0:1], A["L0_attn_time_decay"]),
            (chan[:, 1:2], A["L0_attn_time_first"]),
            (chan[:, 2:3], A["L0_attn_time_mix"].rearrange("a b c -> c (a b)")),
            (k0_u[:, :, :], A["L0_ffn_k0"].rearrange("(k p) f -> p k f", p=P)),
        ]
        loads_a += [(scal[:, i:i + 1], A["L0_ffn_" + n].partition_broadcast(P)) for i, n in enumerate(("s0", "s1", "s2"))]
        loads_a += [
            (k1_u[:, :, :], A["L0_ffn_k1"].rearrange("(k p) f -> p k f", p=P)),
            (k2_u[:, :, :], A["L0_ffn_k2"].rearrange("(k p) f -> p k f", p=P)),
        ]
        loads_b = [
            (w_in[:, :], A["L1_attn_W_in"]),
            (cw[:, :, :], A["L1_attn_conv_w"].rearrange("(k p) a t -> p k (a t)", p=P)),
            (cb[:, :], A["L1_attn_conv_b"].rearrange("(k p) -> p k", p=P)),
            (bdt[:, :], A["L1_attn_b_dt"].rearrange("(k p) -> p k", p=P)),
            (wx[:, :, :], A["L1_attn_W_x"].rearrange("(k p) m -> p k m", p=P)),
            (wdt[:, :], A["L1_attn_W_dt"]),
            (w_out[:, :, :], A["L1_attn_W_out"].rearrange("(k p) m -> p k m", p=P)),
            (up_n[:, 0, :], A["L1_ffn_shared_up"].rearrange("s e h -> (s e) h")),
            (up_n[:, 1:UC, :], A["L1_ffn_routed_up"].rearrange("(k r) e h -> (r e) k h", r=P // E)),
            (dn_n[:, 0, :].rearrange("h (s e) -> h s e", e=E), A["L1_ffn_shared_down"].rearrange("s h e -> h s e")),
            (dn_n[:, 1:UC, :].rearrange("h k (r e) -> h (k r) e", e=E),
             A["L1_ffn_routed_down"].rearrange("r h e -> h r e")),
            (rw_n[:, :], A["L1_ffn_router_w"]),
        ]
        WA_ALL, WB_ALL = 16 * len(loads_a), 16 * len(loads_b)

        up_b = [[(up_n[:, c, :], P) for c in range(b, min(b + 4, UC))] for b in range(0, UC, 4)]
        dn_b = [[(dn_n[:, c, :], P) for c in range(b, min(b + 4, UC))] for b in range(0, UC, 4)]
        up_b[-1].append((rw_n[:, :], NR))
        dn_b[-1] += [(wx[:, k, 0:DS], P) for k in range(IC)]
        batches = up_b + dn_b
        UB, NB = len(up_b), len(up_b) + len(dn_b)
        assert len(up_b[-1]) == 2 and len(dn_b[-1]) == 1 + IC

        b_T, b_K, b_V, b_RX, b_Z0, b_Z1, b_S, b_F = bank
        q_T, q_Q, _, _, _, _, q_S, q_F = bank
        q_D = (bank[2], bank[3])
        q_U = (bank[4], bank[5])
        b_Z = (b_Z0, b_Z1)

        block = ctx.enter_context(nc.Block())

        def after(eng, semaphore, value):
            if not (isinstance(value, int) and value <= 0):
                eng.wait_ge(semaphore, value)

        def has(n):
            return not isinstance(n, int) or 0 <= n < G

        def at_most(n):
            return min(n, G) if isinstance(n, int) else n

        def bodies(eng, body, between=None):
            body(0)
            body(1)
            if between:
                between()
            body(2)
            with eng.Fori(3, G - 1) as n:
                body(n)
            for n in range(G - 1, G + 2):
                body(n)

        def xs_of(n):
            return x_all[:, bass.ds(n * N, N)]

        def seqs(ap):
            return ap.rearrange("p (s t) -> p s t", s=SEQ)

        @block.sync
        def _(sp):
            sp.dma_start(xs_of(0), x_d[0]).then_inc(sem["x_loaded"], 16)
            for dst, src in loads_b:
                sp.dma_start(dst, src, allow_slow_non_contiguous=dst.shape[1] == IC).then_inc(sem["wb_loaded"], 16)
            with sp.Fori(1, G) as n:
                sp.wait_ge(sem["x_loaded"], n * 16)
                sp.dma_start(xs_of(n), x_d[bass.ds(n, 1)].rearrange("g p f -> (g p) f")).then_inc(sem["x_loaded"], 16)
            with sp.Fori(0, G) as n:
                sp.wait_ge(sem["b_out"], n + 1)
                sp.dma_start(out_d[bass.ds(n, 1)].rearrange("g p f -> (g p) f"), xs_of(n)).then_inc(sem["stored"], 16)
            sp.wait_ge(sem["stored"], 16 * G)

        @block.gpsimd
        def _(pool):
            g = nc.gpsimd
            g.memset(ident[:, :], 0.0).then_inc(sem["const_ready"], 1)
            pool.wait_ge(sem["const_ready"], 1)
            g.affine_select(out=ident[:, :], in_=ident[:, :], compare_op=ALU.not_equal, fill=1.0, base=0,
                            pattern=[[-1, P]], channel_multiplier=1).then_inc(sem["ident_ready"], 1)
            g.memset(epsc[:, :], EPS).then_inc(sem["const_ready"], 1)
            g.memset(neghalf[:, :], -0.5).then_inc(sem["const_ready"], 1)
            pool.wait_ge(sem["const_ready"], 3)

            def normalise(n, ph):
                pool.wait_ge(sem[ph + "stat"], n + 1)
                g.tensor_tensor(ve[:, :], mv[:, :, 1], epsc[:, :], ALU.add).then_inc(sem[ph + "vareps"], 1)
                pool.wait_ge(sem[ph + "vareps"], n + 1)
                g.tensor_tensor(rstd[:, :], ve[:, :], neghalf[:, :], ALU.pow).then_inc(sem[ph + "rstd"], 1)
                after(pool, sem[ph + "xnT"], n)
                g.tensor_tensor(xn[:, :, :], xs_of(n).rearrange("p (j c) -> p j c", j=J),
                                mv[:, :, 0:1].to_broadcast([P, J, P]), ALU.subtract).then_inc(sem[ph + "centred"], 1)
                pool.wait_ge(sem[ph + "rstd"], n + 1)
                pool.wait_ge(sem[ph + "centred"], n + 1)
                g.tensor_tensor(xn[:, :, :], xn[:, :, :], rstd[:, :].unsqueeze(2).to_broadcast([P, J, P]),
                                ALU.mult).then_inc(sem[ph + "xn"], 1)

            normalise(0, "a_")
            g.memset(ones[:, :], 1.0).then_inc(sem["const_ready"], 1)
            g.memset(prev[:, :, 0:1], 0.0).then_inc(sem["const_ready"], 1)
            g.memset(Pk[:, :, 0:1], 0.0).then_inc(sem["const_ready"], 1)
            g.memset(Pv[:, :, 0:1], 0.0).then_inc(sem["const_ready"], 1)
            g.memset(amax[:, :], 0.0).then_inc(sem["const_ready"], 1)
            g.memset(xi[:, :, :, 0:TAPS - 1], 0.0).then_inc(sem["const_ready"], 1)
            g.memset(pe_[:, :, NR:], -1.0).then_inc(sem["const_ready"], 1)

            def layer0(n):
                f, m = n, n - 1
                if has(m):
                    pool.wait_ge(sem["a_rec"], m + 1)
                    pool.wait_ge(sem["a_ysr"], m + 1)
                    after(pool, sem["a_s"], m)
                    g.tensor_tensor(ya[:, :], ysr[:, :], rec[:, :], ALU.mult).then_inc(sem["a_y"], 1)
                if has(f) and has(f + 1):
                    normalise(f + 1, "a_")
                if has(f):
                    pool.wait_ge(sem["a_wkc"], f + 1)
                    pool.wait_ge(sem["a_scanK"], f + 1)
                    g.tensor_tensor(seqs(wk[:, :]), seqs(wkc[:, :]), Pk[:, :, 0:T], ALU.add).then_inc(sem["a_wk"], 1)
                    pool.wait_ge(sem["a_kvc"], f + 1)
                    pool.wait_ge(sem["a_scanV"], f + 1)
                    g.tensor_tensor(seqs(wkv[:, :]), seqs(kvc[:, :]), Pv[:, :, 0:T], ALU.add).then_inc(sem["a_wkv"], 1)
                    pool.wait_ge(sem["a_wkv"], f + 1)
                    pool.wait_ge(sem["a_sr"], f + 1)
                    g.tensor_tensor(ysr[:, :], wkv[:, :], sr[:, :], ALU.mult).then_inc(sem["a_ysr"], 1)

            def weights():
                g.memset(sel[:, :, :], 0.0).then_inc(sem["sel_ready"], 1)
                for b in range(3):
                    pool.wait_ge(sem["sel_ready"], b + 1)
                    v = sel[:, :, :].rearrange("k c (h e) -> k c h e", e=E)
                    g.affine_select(out=v, in_=v, compare_op=ALU.not_equal, fill=1.0, base=-NR * b,
                                    pattern=[[-(P // E), RC], [-1, P // E], [0, E]],
                                    channel_multiplier=1).then_inc(sem["sel_ready"], 1)
                g.tensor_copy(identb[:, :], ident[:, :]).then_inc(sem["ident_ready"], 1)
                pool.wait_ge(sem["absmax_ready"], 3)
                g.partition_all_reduce(amax[:, :], amax[:, :], P, bass.bass_isa.ReduceOp.max).then_inc(sem["absmax_all"], 1)

            bodies(pool, layer0, weights)

            def layer1(n):
                f, m = n, n - 1
                if has(f) and has(f + 1):
                    normalise(f + 1, "b_")
                if has(m):
                    for k in range(IC):
                        pool.wait_ge(sem["b_cr"], IC * m + k + 1)
                        pool.wait_ge(sem["b_scan"], IC * m + k + 1)
                        after(pool, sem["b_s"], m)
                        g.tensor_tensor(yb[:, k, :], H[:, k, :], cr[:, k, :], ALU.mult).then_inc(sem["b_y"], 1)

            normalise(0, "b_")
            bodies(pool, layer1)

        @block.scalar
        def _(actv):
            a = nc.scalar
            for dst, src in loads_a:
                actv.dma_start(dst, src).then_inc(sem["wa_loaded"], 16)
            actv.wait_ge(sem["wa_loaded"], WA_ALL)
            a.activation(sg_[:, :], scal[:, 0:2], ACT.Sign).then_inc(sem["signs_ready"], 1)
            a.activation(tch[:, 0:1], chan[:, 0:1], ACT.Exp).then_inc(sem["chan_ready"], 1)
            actv.wait_ge(sem["chan_ready"], 1)
            a.activation(tch[:, 1:2], tch[:, 0:1], ACT.Exp, scale=-1.0).then_inc(sem["chan_ready"], 1)
            a.activation(tch[:, 2:3], chan[:, 1:2], ACT.Exp).then_inc(sem["chan_ready"], 1)
            actv.wait_ge(sem["chan_ready"], 3)
            actv.wait_ge(sem["const_done"], 1)

            def high(layer, n, j):
                actv.wait_ge(sem[("a_z0", "a_z1")[layer]], FC * n + j + 1)
                if layer:
                    after(actv, sem["a_f"], n)
                a.activation(hh[:, layer, j, :], b_Z[j % 2][:, :], ACT.Relu).then_inc(sem[("a_hi0", "a_hi1")[layer]], 1)

            def layer0(n):
                f, m = n, n - 1
                if has(f):
                    actv.wait_ge(sem["a_xnT"], f + 1)
                    after(actv, sem["a_xm"], f)
                    a.activation(prev[:, :, 1:T], seqs(b_T[:, :])[:, :, 0:T - 1], ACT.Copy,
                                 scale=tch[:, 3:4]).then_inc(sem["a_prev"], 1)
                    after(actv, sem["a_z0"], FC * f)
                    a.activation(xh[:, :], b_T[:, :], ACT.Copy, scale=XS).then_inc(sem["a_xh"], 1)
                if has(m):
                    high(1, m, 0)
                    high(1, m, 1)
                if has(f):
                    actv.wait_ge(sem["a_k"], f + 1)
                    after(actv, sem["a_ekm"], f)
                    a.activation(ek[:, :], b_K[:, :], ACT.Exp).then_inc(sem["a_ek"], 1)
                if has(m):
                    high(1, m, 2)
                if has(f):
                    actv.wait_ge(sem["a_ekm"], f + 1)
                    after(actv, sem["a_wk"], f)
                    a.activation(wkc[:, :], ekm[:, :], ACT.Copy, scale=tch[:, 2:3], bias=WK_EPS).then_inc(sem["a_wkc"], 1)
                if has(m):
                    high(1, m, 3)
                if has(f):
                    actv.wait_ge(sem["a_kv"], f + 1)
                    after(actv, sem["a_wkv"], f)
                    a.activation(kvc[:, :], kv[:, :], ACT.Copy, scale=tch[:, 2:3]).then_inc(sem["a_kvc"], 1)
                    actv.wait_ge(sem["a_r"], f + 1)
                    a.activation(thr[:, :], b_RX[:, :], ACT.Tanh, scale=0.5).then_inc(sem["a_thr"], 1)
                    high(0, f, 0)
                    actv.wait_ge(sem["a_thr"], f + 1)
                    after(actv, sem["a_ysr"], f)
                    a.activation(sr[:, :], thr[:, :], ACT.Copy, scale=0.5, bias=0.5).then_inc(sem["a_sr"], 1)
                    high(0, f, 1)
                if has(m):
                    actv.wait_ge(sem["a_f"], m + 1)
                    after(actv, sem["a_gp"], m)
                    a.activation(thf[:, :], b_F[:, :], ACT.Tanh, scale=c3[:, 2:3]).then_inc(sem["a_thf"], 1)
                if has(f):
                    high(0, f, 2)
                    high(0, f, 3)

            def weights():
                actv.wait_ge(sem["pow2_ready"], 1)
                for i in range(UB):
                    actv.wait_ge(sem["prep_turned"], i + 1)
                    w = min(UC * P - 4 * i * P, 4 * P)
                    last = a.activation(upH[:, 4 * i * P:4 * i * P + w], (b_K, b_V)[i % 2][:, 0:w], ACT.Copy,
                                        scale=wsc[:, 1:2])
                    if i == UB - 1:
                        last = a.activation(rwH[:, :], (b_K, b_V)[i % 2][:, w:w + NR], ACT.Copy, scale=wsc[:, 2:3])
                    last.then_inc(sem["prep_high"], 1)

            bodies(actv, layer0, weights)

            GELU_SET, EXP_SET = "gelu_and_others", "natural_log_exp_and_others"

            def layer1(n):
                f, m, t = n, n - 1, n - 2
                if has(t):
                    actv.wait_ge(sem["b_down"], t + 1)
                    after(actv, sem["b_gp"], t)
                    a.activation(thf[:, :], q_F[:, :], ACT.Tanh, scale=0.5).then_inc(sem["b_thf"], 1)
                if has(f):
                    actv.wait_ge(sem["b_xnT"], f + 1)
                    after(actv, sem["b_up"], UC * f)
                    a.activation(xh[:, :], q_T[:, :], ACT.Copy, scale=XS).then_inc(sem["b_xh"], 1)
                if has(m):
                    a.preload_act_table_set(EXP_SET)
                    actv.wait_ge(sem["b_lg"], m + 1)
                    after(actv, sem["b_gt"], m)
                    a.activation(pe_[:, :, 0:NR], lg[:, :, :], ACT.Exp, scale=inv[:, 2:3]).then_inc(sem["b_pe"], 1)
                for k in range(IC):
                    if has(f):
                        actv.wait_ge(sem["b_xin"], IC * f + k + 1)
                        after(actv, sem["b_conv"], IC * f * (TAPS - 1))
                        after(actv, sem["b_xc2"], IC * f)
                        a.activation(xi[:, k, :, TAPS - 1:], seqs(q_U[k][:, :]), ACT.Copy, scale=inv[:, 0:1])
                        a.activation(u[:, k, :], q_U[k][:, :], ACT.Identity, scale=cwi[:, k:k + 1],
                                     bias=cb[:, k:k + 1]).then_inc(sem["b_u0"], 1)
                    if has(m):
                        actv.wait_ge(sem["b_d"], IC * m + k + 1)
                        after(actv, sem["b_em"], IC * m)
                        a.activation(e_[:, k, :], q_D[k][:, :], ACT.Exp, bias=bdt[:, k:k + 1]).then_inc(sem["b_e"], 1)
                if has(m):
                    for k in range(IC):
                        actv.wait_ge(sem["b_em"], IC * m + k + 1)
                        after(actv, sem["b_delta"], IC * m)
                        a.activation(lnv[:, k, :], em[:, k, :], ACT.Ln, bias=1.0).then_inc(sem["b_ln"], 1)
                a.preload_act_table_set(GELU_SET)
                if has(f):
                    for k in range(IC):
                        actv.wait_ge(sem["b_res"], IC * f + k + 1)
                        after(actv, sem["b_r2"], IC * f)
                        a.activation(th2[:, k, :], (q_T, q_S)[k][:, :], ACT.Tanh, scale=hinv[:, 0:1]).then_inc(sem["b_thr"], 1)
                if has(m):
                    actv.wait_ge(sem["b_gtT"], m + 1)
                    after(actv, sem["b_gate"], RC * m)
                    a.copy(gT[:, :].rearrange("r (p j) -> r j p", j=J),
                           q_Q[0:3 * NR, 0:N // 2].bitcast(BF16).rearrange("r (j p) -> r j p", j=J)).then_inc(sem["b_gT"], 1)
                if has(f):
                    for c in range(UC):
                        actv.wait_ge(sem["b_up"], UC * f + c + 1)
                        a.activation(act[:, c, :], q_U[c % 2][:, :], ACT.Gelu, scale=inv[:, 1:2]).then_inc(sem["b_act"], 1)
                        if c in (4, UC - 1):
                            k = 0 if c == 4 else 1
                            actv.wait_ge(sem["b_conv"], (IC * f + k + 1) * (TAPS - 1))
                            a.activation(thu[:, k, :], u[:, k, :], ACT.Tanh, scale=0.5).then_inc(sem["b_thu"], 1)

            bodies(actv, layer1)

        @block.vector
        def _(dve):
            v = nc.vector
            steps = [0]

            def link(ins):
                steps[0] += 1
                ins.then_inc(sem["chain"], 1)
                dve.wait_ge(sem["chain"], steps[0])

            def row_stats(n):
                for j in range(J):
                    last = v.bn_stats(st[:, j, :], x_all[:, bass.ds(n * N + j * P, P)])
                last.then_inc(sem["bn_done"], 1)

            def row_moments(ready):
                for j in range(J):
                    last = v.bn_aggr(mv[:, j, :], st[:, j, :])
                last.then_inc(ready, 1)

            dve.wait_ge(sem["x_loaded"], 16)
            row_stats(0)
            dve.wait_ge(sem["bn_done"], 1)
            row_moments(sem["a_stat"])
            dve.wait_ge(sem["square_turned"], 1)
            v.tensor_copy(wsqT[:, :, :].rearrange("p a b -> p (a b)"), b_S[:, :]).then_inc(sem["square_ready"], 1)
            dve.wait_ge(sem["wa_loaded"], WA_ALL)
            dve.wait_ge(sem["signs_ready"], 1)
            link(v.tensor_scalar(tch[:, 3:4], chan[:, 2:3], -1.0, 1.0, ALU.mult, ALU.add))
            link(v.tensor_scalar(w0c[:, :], sg_[:, 0:1], 2.0 * W0S, None, ALU.mult))
            link(v.tensor_tensor(w0d[:, :], k0_u[:, 0, :], k0_u[:, 1, :], ALU.subtract))
            link(v.tensor_scalar(w0[:, :], w0d[:, :], w0c[:, 0:1], None, ALU.mult))
            link(v.tensor_scalar(w1c[:, 0:1], sg_[:, 1:2], 2.0 * W1S, None, ALU.mult))
            link(v.tensor_scalar(w1c[:, 1:2], sg_[:, 1:2], -W1S, None, ALU.mult))
            link(v.tensor_tensor(sab[:, :], scal[:, 0:2], sg_[:, :], ALU.mult))
            link(v.tensor_tensor(c3[:, 0:1], sab[:, 0:1], sab[:, 1:2], ALU.mult))
            link(v.scalar_tensor_tensor(c3[:, 1:2], c3[:, 0:1], FS, scal[:, 2:3], ALU.mult, ALU.mult))
            link(v.tensor_scalar(c3[:, 2:3], c3[:, 1:2], 0.5, None, ALU.mult))
            dve.wait_ge(sem["const_ready"], 7)
            dve.wait_ge(sem["chan_ready"], 3)
            link(v.tensor_scalar(dec[:, 0:P], ones[:, :], tch[:, 1:2], None, ALU.mult))
            link(v.tensor_scalar(dec[:, P:T], ones[:, 0:T - P], tch[:, 1:2], None, ALU.mult))
            v.tensor_scalar(w1[:, :, :], k1_u[:, :, :], w1c[:, 0:1], w1c[:, 1:2], ALU.mult, ALU.add)
            v.tensor_scalar(w2[:, :, :], k2_u[:, :, :], 2.0, -1.0, ALU.mult, ALU.add).then_inc(sem["const_done"], 1)

            def low(layer, n, j):
                dve.wait_ge(sem[("a_hi0", "a_hi1")[layer]], FC * n + j + 1)
                v.scalar_tensor_tensor(hl[:, layer, j, :], b_Z[j % 2][:, :], 0.0, hh[:, layer, j, :],
                                       ALU.max, ALU.subtract).then_inc(sem[("a_lo0", "a_lo1")[layer]], 1)

            def layer0(n):
                f, m, t = n, n - 1, n - 2
                ahead = has(f) and has(f + 1)
                if has(f):
                    dve.wait_ge(sem["a_xh"], f + 1)
                    after(dve, sem["a_r"], f)
                    v.scalar_tensor_tensor(xm[:, :], b_T[:, :], chan[:, 2:3], prev[:, :, :].rearrange("p s t -> p (s t)"),
                                           ALU.mult, ALU.add).then_inc(sem["a_xm"], 1)
                    if ahead:
                        dve.wait_ge(sem["x_loaded"], f * 16 + 32)
                        row_stats(f + 1)
                        dve.wait_ge(sem["a_xn"], f + 1)
                        dve.wait_ge(sem["bn_done"], f + 2)
                    after(dve, sem["a_z0"], FC * f)
                    v.scalar_tensor_tensor(xl[:, :], b_T[:, :], XS, xh[:, :], ALU.mult, ALU.subtract).then_inc(sem["a_xl"], 1)
                    if ahead:
                        row_moments(sem["a_stat"])
                if has(m):
                    low(1, m, 0)
                    dve.wait_ge(sem["a_wk"], m + 1)
                    after(dve, sem["a_y"], m)
                    v.reciprocal(rec[:, 0:N // 2], wk[:, 0:N // 2])
                    low(1, m, 1)
                if has(t):
                    dve.wait_ge(sem["a_sgT"], t + 1)
                    v.tensor_tensor(xs_of(t), xs_of(t), b_RX[:, :], ALU.add).then_inc(sem["a_x1"], 1)
                if has(m):
                    v.reciprocal(rec[:, N // 2:], wk[:, N // 2:]).then_inc(sem["a_rec"], 1)
                if has(f):
                    dve.wait_ge(sem["a_ek"], f + 1)
                    after(dve, sem["a_wkc"], f)
                    v.tensor_scalar(ekm[:, :], ek[:, :], math.exp(K_CAP), None, ALU.min).then_inc(sem["a_ekm"], 1)
                    dve.wait_ge(sem["a_ekm"], f + 1)
                    dve.wait_ge(sem["a_v"], f + 1)
                    after(dve, sem["a_kvc"], f)
                    v.tensor_tensor(kv[:, :], ekm[:, :], b_V[:, :], ALU.mult).then_inc(sem["a_kv"], 1)
                if has(m):
                    low(1, m, 2)
                if has(f):
                    after(dve, sem["a_wk"], f)
                    for s in range(SEQ):
                        last = v.tensor_tensor_scan(Pk[:, s, 1:], dec[:, :], ekm[:, s * T:(s + 1) * T], 0.0,
                                                    ALU.mult, ALU.add)
                    last.then_inc(sem["a_scanK"], 1)
                if has(m):
                    low(1, m, 3)
                if has(f):
                    dve.wait_ge(sem["a_kv"], f + 1)
                    after(dve, sem["a_wkv"], f)
                    for s in range(SEQ):
                        last = v.tensor_tensor_scan(Pv[:, s, 1:], dec[:, :], kv[:, s * T:(s + 1) * T], 0.0,
                                                    ALU.mult, ALU.add)
                    last.then_inc(sem["a_scanV"], 1)
                    low(0, f, 0)
                    low(0, f, 1)
                if has(m):
                    dve.wait_ge(sem["a_thf"], m + 1)
                    after(dve, sem["a_sg"], m)
                    v.scalar_tensor_tensor(gp[:, :], thf[:, :], 1.0, b_F[:, :], ALU.add, ALU.mult).then_inc(sem["a_gp"], 1)
                if has(f):
                    low(0, f, 2)
                    low(0, f, 3)
                if has(m):
                    dve.wait_ge(sem["a_gp"], m + 1)
                    dve.wait_ge(sem["a_s"], m + 1)
                    after(dve, sem["a_sgT"], m)
                    v.scalar_tensor_tensor(sg[:, :], b_S[:, :], c3[:, 2:3], gp[:, :], ALU.mult, ALU.mult).then_inc(sem["a_sg"], 1)

            def weights():
                dve.wait_ge(sem["wb_loaded"], WB_ALL)
                dve.wait_ge(sem["const_ready"], 10)
                for i, w in enumerate((w_in[:, :], up_n[:, :, :].rearrange("p a b -> p (a b)"), rw_n[:, :])):
                    v.tensor_reduce(amax[0:w.shape[0], i:i + 1], w, AX.X, ALU.max,
                                    apply_absolute_value=True).then_inc(sem["absmax_ready"], 1)
                link(v.tensor_scalar(wc[:, :, :], wx[:, :, 2 * DS:], 0.5, None, ALU.mult))
                link(v.tensor_reduce(wbs[:, :], wx[:, :, DS:2 * DS], AX.X, ALU.add))
                for k in range(IC):
                    link(v.tensor_scalar(wb[:, k, :], ones[:, :], wbs[:, k:k + 1], 0.25, ALU.mult, ALU.mult))
                dve.wait_ge(sem["absmax_all"], 1)
                link(v.tensor_scalar(amax[:, :], amax[:, :], 1e-30, None, ALU.max))
                link(v.tensor_scalar(pow2[:, :].bitcast(mybir.dt.int32), amax[:, :].bitcast(mybir.dt.int32), 0x7F800000,
                                     None, ALU.bitwise_and))
                link(v.tensor_scalar(inv[:, :], pow2[:, :], 2.0 ** -13, None, ALU.mult))
                link(v.reciprocal(wsc[:, :], inv[:, :]))
                link(v.tensor_scalar(inv[:, :], inv[:, :], 1.0 / XS, None, ALU.mult))
                link(v.tensor_scalar(hinv[:, :], inv[:, 0:1], 0.5, None, ALU.mult))
                v.tensor_scalar(cwi[:, :], cw[:, :, TAPS - 1], inv[:, 0:1], None, ALU.mult).then_inc(sem["pow2_ready"], 1)
                link(v.tensor_scalar(w_inH[:, :], w_in[:, :], wsc[:, 0:1], None, ALU.mult))
                v.scalar_tensor_tensor(w_inL[:, :], w_in[:, :], wsc[:, 0:1], w_inH[:, :], ALU.mult,
                                       ALU.subtract).then_inc(sem["prep_sbuf"], 1)
                for i in range(NB + 1):
                    ps = (b_K, b_V)[i % 2]
                    if i < UB:
                        w = min(UC * P - 4 * i * P, 4 * P)
                        cut = slice(4 * i * P, 4 * i * P + w)
                        dve.wait_ge(sem["prep_high"], i + 1)
                        last = v.scalar_tensor_tensor(upL[:, cut], ps[:, 0:w], wsc[:, 1:2], upH[:, cut], ALU.mult, ALU.subtract)
                        if i == UB - 1:
                            last = v.scalar_tensor_tensor(rwL[:, :], ps[:, w:w + NR], wsc[:, 2:3], rwH[:, :],
                                                          ALU.mult, ALU.subtract)
                    elif i < NB:
                        c = 4 * (i - UB)
                        w = min(UC - c, 4)
                        dve.wait_ge(sem["prep_turned"], i + 1)
                        last = v.tensor_copy(dnT[:, c:c + w, :].rearrange("p a b -> p (a b)"), ps[:, 0:w * P])
                        if i == NB - 1:
                            last = v.tensor_copy(wxsT[:, :, :].rearrange("p a b -> p (a b)"), ps[0:DS, w * P:w * P + IC * P])
                    else:
                        dve.wait_ge(sem["prep_turned"], i + 1)
                        last = v.tensor_scalar(wdel[:, :, :].rearrange("p a b -> p (a b)"), ps[:, 0:IC * DI], 0.5, None, ALU.mult)
                    last.then_inc(sem["prep_out"], 1)

            bodies(dve, layer0, weights)

            def top_four(n):
                dve.wait_ge(sem["b_pe"], n + 1)
                v.reduce_sum(sm[:, :], pe_[:, :, 0:NR], AX.X).then_inc(sem["b_sum"], 1)
                for j in range(J):
                    last = v.max(top[:, j, :], pe_[:, j, 0:NR])
                last.then_inc(sem["b_top"], 1)
                dve.wait_ge(sem["b_top"], n + 1)
                v.memset(top[:, :, TOP_K:], -1.0).then_inc(sem["b_fill"], 1)
                dve.wait_ge(sem["b_sum"], n + 1)
                dve.wait_ge(sem["b_fill"], n + 1)
                v.reciprocal(rs[:, :], sm[:, :]).then_inc(sem["b_rs"], 1)
                for j in range(J):
                    last = v.match_replace(rep[:, j, :], top[:, j, :], pe_[:, j, :], 0.0)
                last.then_inc(sem["b_rep"], 1)

            def gates(n):
                dve.wait_ge(sem["b_rep"], n + 1)
                v.tensor_tensor(gt[:, :, :], pe_[:, :, 0:NR], rep[:, :, 0:NR], ALU.subtract).then_inc(sem["b_gt"], 1)
                dve.wait_ge(sem["b_gt"], n + 1)
                dve.wait_ge(sem["b_rs"], n + 1)
                v.tensor_tensor(gn[:, :, :], gt[:, :, :], rs[:, :].unsqueeze(2).to_broadcast([P, J, NR]),
                                ALU.mult).then_inc(sem["b_gn"], 1)
                dve.wait_ge(sem["b_gn"], n + 1)
                after(dve, sem["b_gtT"], n)
                v.tensor_copy(g3[:, :, 0, :], gn[:, :, :]).then_inc(sem["b_g1"], 1)
                dve.wait_ge(sem["b_g1"], n + 1)
                v.tensor_tensor(gr[:, :, :], gn[:, :, :], g3[:, :, 0, :], ALU.subtract).then_inc(sem["b_g2"], 1)
                dve.wait_ge(sem["b_g2"], n + 1)
                v.tensor_copy(g3[:, :, 1, :], gr[:, :, :]).then_inc(sem["b_g3"], 1)
                dve.wait_ge(sem["b_g3"], n + 1)
                v.tensor_tensor(g3[:, :, 2, :], gr[:, :, :], g3[:, :, 1, :], ALU.subtract).then_inc(sem["b_g4"], 1)

            def conv(n, k, t):
                i = (IC * n + k) * (TAPS - 1) + t
                if t == 0:
                    dve.wait_ge(sem["b_u0"], IC * n + k + 1)
                else:
                    dve.wait_ge(sem["b_conv"], i)
                uk = seqs(u[:, k, :])
                v.scalar_tensor_tensor(uk, xi[:, k, :, t:t + T], cw[:, k, t:t + 1], uk, ALU.mult, ALU.add)\
                    .then_inc(sem["b_conv"], 1)

            def layer1(n):
                f, m, t = n, n - 1, n - 2
                ahead = has(f) and has(f + 1)
                if has(t):
                    dve.wait_ge(sem["b_thf"], t + 1)
                    v.scalar_tensor_tensor(gp[:, :], thf[:, :], 1.0, q_F[:, :], ALU.add, ALU.mult).then_inc(sem["b_gp"], 1)
                    dve.wait_ge(sem["b_gp"], t + 1)
                    dve.wait_ge(sem["b_s"], t + 1)
                    after(dve, sem["b_sgT"], t)
                    v.scalar_tensor_tensor(sg[:, :], q_S[:, :], 0.5, gp[:, :], ALU.mult, ALU.mult).then_inc(sem["b_sg"], 1)
                if has(f):
                    dve.wait_ge(sem["b_xh"], f + 1)
                    after(dve, sem["b_up"], UC * f)
                    v.scalar_tensor_tensor(xl[:, :], q_T[:, :], XS, xh[:, :], ALU.mult, ALU.subtract).then_inc(sem["b_xl"], 1)
                if has(m):
                    for k in range(IC):
                        dve.wait_ge(sem["b_c"], IC * m + k + 1)
                        after(dve, sem["b_y"], IC * m)
                        v.scalar_tensor_tensor(cr[:, k, :], q_U[k][:, :], inv[:, 0:1], r2[:, k, :],
                                               ALU.mult, ALU.mult).then_inc(sem["b_cr"], 1)
                    top_four(m)
                if has(f):
                    lp = q_Q[:, 0:J * NR].rearrange("p (j r) -> p j r", r=NR)
                    dve.wait_ge(sem["b_rout"], f + 1)
                    v.tensor_reduce(mx[:, :], lp, AX.X, ALU.max).then_inc(sem["b_mx"], 1)
                    dve.wait_ge(sem["b_mx"], f + 1)
                    after(dve, sem["b_pe"], f)
                    v.tensor_tensor(lg[:, :, :], lp, mx[:, :].unsqueeze(2).to_broadcast([P, J, NR]),
                                    ALU.subtract).then_inc(sem["b_lg"], 1)
                if has(m):
                    gates(m)
                    for k in range(IC):
                        dve.wait_ge(sem["b_e"], IC * m + k + 1)
                        v.tensor_scalar(em[:, k, :], e_[:, k, :], math.exp(SP_CAP), None, ALU.min).then_inc(sem["b_em"], 1)
                if has(m):
                    for k in range(IC):
                        dve.wait_ge(sem["b_ln"], IC * m + k + 1)
                        v.scalar_tensor_tensor(delta[:, k, :], q_D[k][:, :], bdt[:, k:k + 1], lnv[:, k, :],
                                               ALU.add, ALU.max).then_inc(sem["b_delta"], 1)
                if has(t):
                    dve.wait_ge(sem["b_sgT"], t + 1)
                    v.tensor_tensor(xs_of(t), xs_of(t), q_Q[:, :], ALU.add).then_inc(sem["b_out"], 1)
                if has(f):
                    for k in range(IC):
                        dve.wait_ge(sem["b_thr"], IC * f + k + 1)
                        v.scalar_tensor_tensor(r2[:, k, :], th2[:, k, :], 1.0, (q_T, q_S)[k][:, :], ALU.add,
                                               ALU.mult).then_inc(sem["b_r2"], 1)
                    if ahead:
                        row_stats(f + 1)
                for c in range(RC):
                    if has(m):
                        if c == 1 and ahead:
                            dve.wait_ge(sem["b_xn"], f + 1)
                            dve.wait_ge(sem["bn_done"], G + f + 2)
                        dve.wait_ge(sem["b_gate"], RC * m + c + 1)
                        v.tensor_tensor(act[:, c + 1, :], act[:, c + 1, :], q_D[c % 2][:, :], ALU.mult).then_inc(sem["b_actg"], 1)
                    if ahead and c == 1:
                        if not has(m):
                            dve.wait_ge(sem["b_xn"], f + 1)
                            dve.wait_ge(sem["bn_done"], G + f + 2)
                        row_moments(sem["b_stat"])
                    if has(f) and c < IC * (TAPS - 1):
                        conv(f, c // (TAPS - 1), c % (TAPS - 1))
                    if has(m) and c == 2:
                        dve.wait_ge(sem["b_b"], m + 1)
                        for k in range(IC):
                            v.tensor_tensor(bx[:, k, :], xc2[:, k, :], q_T[:, :], ALU.mult).then_inc(sem["b_bx"], 1)
                    if has(m) and c in (3, 4):
                        k = c - 3
                        dve.wait_ge(sem["b_bx"], IC * m + k + 1)
                        dve.wait_ge(sem["b_delta"], IC * m + k + 1)
                        after(dve, sem["b_y"], IC * m)
                        for s in range(SEQ):
                            w = slice(s * T, (s + 1) * T)
                            last = v.tensor_tensor_scan(H[:, k, w], delta[:, k, w], bx[:, k, w], 0.0, ALU.mult, ALU.add)
                        last.then_inc(sem["b_scan"], 1)
                if has(f):
                    for k in range(IC):
                        dve.wait_ge(sem["b_thu"], IC * f + k + 1)
                        after(dve, sem["b_b"], f)
                        v.scalar_tensor_tensor(xc2[:, k, :], thu[:, k, :], 1.0, u[:, k, :], ALU.add,
                                               ALU.mult).then_inc(sem["b_xc2"], 1)

            dve.wait_ge(sem["a_x1"], G)
            dve.wait_ge(sem["a_xn"], G)
            row_stats(0)
            dve.wait_ge(sem["bn_done"], G + 1)
            row_moments(sem["b_stat"])
            bodies(dve, layer1)

        @block.tensor
        def _(pe):
            def mm(ps, lhsT, rhs, start=True, stop=True):
                return nc.tensor.matmul(ps, lhsT, rhs, start=start, stop=stop)

            def split3(ps, wh, wl, h, l):
                mm(ps, wh, h, True, False)
                mm(ps, wh, l, False, False)
                return mm(ps, wl, h, False, True)

            def turn_rows(ps):
                for j in range(J):
                    last = nc.tensor.transpose(ps[:, j::J], xn[:, j, :], ident[:, :])
                return last

            def turn_back(ps):
                for j in range(J):
                    last = nc.tensor.transpose(ps[:, j * P:(j + 1) * P], sg[:, j::J], ident[:, :])
                return last

            pe.wait_ge(sem["wa_loaded"], WA_ALL)
            pe.wait_ge(sem["ident_ready"], 1)
            for i in range(4):
                last = nc.tensor.transpose(b_S[:, i * P:(i + 1) * P], wsq[:, i, :], ident[:, :])
            last.then_inc(sem["square_turned"], 1)

            def layer0(n):
                f, m, t = n, n - 1, n - 2

                def hidden0(j):
                    if j < 2:
                        after(pe, sem["a_lo1"], FC * m + j + 3)
                    else:
                        pe.wait_ge(sem["a_lo0"], FC * f + j - 1)
                    mm(b_Z[j % 2][:, :], w0[:, j * P:(j + 1) * P], xh[:, :], True, False)
                    mm(b_Z[j % 2][:, :], w0[:, j * P:(j + 1) * P], xl[:, :], False, True).then_inc(sem["a_z0"], 1)

                def hidden1(j):
                    if j < 2:
                        pe.wait_ge(sem["a_lo0"], FC * m + FC)
                    else:
                        pe.wait_ge(sem["a_lo1"], FC * m + j - 1)
                    for k in range(FC):
                        w = w1[:, k, j * P:(j + 1) * P]
                        mm(b_Z[j % 2][:, :], w, hh[:, 0, k, :], k == 0, False)
                        last = mm(b_Z[j % 2][:, :], w, hl[:, 0, k, :], False, k == FC - 1)
                    last.then_inc(sem["a_z1"], 1)

                if has(f):
                    pe.wait_ge(sem["a_xn"], f + 1)
                    after(pe, sem["a_xl"], f)
                    turn_rows(b_T).then_inc(sem["a_xnT"], 1)
                if has(m):
                    hidden1(0)
                if has(t):
                    pe.wait_ge(sem["a_sg"], t + 1)
                    pe.wait_ge(sem["a_thr"], at_most(t + 2))
                    turn_back(b_RX).then_inc(sem["a_sgT"], 1)
                if has(m):
                    hidden1(1)
                if has(f):
                    pe.wait_ge(sem["a_xm"], f + 1)
                    if isinstance(f, int) and f == 0:
                        pe.wait_ge(sem["square_ready"], 1)
                    after(pe, sem["a_ek"], f)
                    if isinstance(f, int) and f == 2:
                        pe.wait_ge(sem["prep_out"], NB + 1)
                    mm(b_K[:, :], wsqT[:, 0, :], xm[:, :]).then_inc(sem["a_k"], 1)
                    after(pe, sem["a_kv"], f)
                    mm(b_V[:, :], wsqT[:, 1, :], xm[:, :]).then_inc(sem["a_v"], 1)
                if has(m):
                    hidden1(2)
                    hidden1(3)
                if has(f):
                    if has(t):
                        pe.wait_ge(sem["a_x1"], t + 1)
                    mm(b_RX[:, :], wsqT[:, 2, :], xm[:, :]).then_inc(sem["a_r"], 1)
                    pe.wait_ge(sem["a_xl"], f + 1)
                    if isinstance(f, int) and f == 0:
                        pe.wait_ge(sem["const_done"], 1)
                    hidden0(0)
                    hidden0(1)
                if has(m):
                    after(pe, sem["a_gp"], m)
                    for k in range(FC):
                        pe.wait_ge(sem["a_lo1"], FC * m + k + 1)
                        mm(b_F[:, :], w2[:, k, :], hh[:, 1, k, :], k == 0, False)
                        last = mm(b_F[:, :], w2[:, k, :], hl[:, 1, k, :], False, k == FC - 1)
                    last.then_inc(sem["a_f"], 1)
                if has(f):
                    hidden0(2)
                    hidden0(3)
                if has(m):
                    pe.wait_ge(sem["a_y"], m + 1)
                    after(pe, sem["a_sg"], m)
                    mm(b_S[:, :], wsqT[:, 3, :], ya[:, :]).then_inc(sem["a_s"], 1)

            def weights():
                pe.wait_ge(sem["wb_loaded"], WB_ALL)
                pe.wait_ge(sem["a_ek"], 2)
                pe.wait_ge(sem["a_kv"], 2)
                for i, batch in enumerate(batches):
                    if i >= 2:
                        pe.wait_ge(sem["prep_out"], i - 1)
                    col = 0
                    for src, width in batch:
                        rows, cols = src.shape[0], src.shape[1]
                        last = nc.tensor.transpose((b_K, b_V)[i % 2][0:cols, col:col + rows], src, ident[0:rows, 0:rows])
                        col += rows
                    last.then_inc(sem["prep_turned"], 1)
                pe.wait_ge(sem["prep_out"], NB)
                for k in range(IC):
                    last = mm((b_K, b_V)[NB % 2][:, k * DI:(k + 1) * DI], wxsT[:, k, :], wdt[:, :])
                last.then_inc(sem["prep_turned"], 1)

            bodies(pe, layer0, weights)

            def layer1(n):
                f, m, t = n, n - 1, n - 2
                if has(f):
                    pe.wait_ge(sem["b_xn"], f + 1)
                    after(pe, sem["b_bx"], IC * m)
                    turn_rows(q_T).then_inc(sem["b_xnT"], 1)
                if has(m):
                    pe.wait_ge(sem["b_xc2"], IC * m + IC)
                    pe.wait_ge(sem["b_act"], UC * m + UC)
                    for i in range(IC):
                        for k in range(IC):
                            last = mm(q_U[i][:, :], wc[:, k, i * P:(i + 1) * P], xc2[:, k, :], k == 0, k == IC - 1)
                        last.then_inc(sem["b_c"], 1)
                for i in range(IC):
                    if has(f):
                        pe.wait_ge(sem["b_xl"], f + 1)
                        if has(m):
                            pe.wait_ge(sem["b_cr"], IC * m + i + 1)
                        w = slice(i * P, (i + 1) * P)
                        split3(q_U[i][:, :], w_inH[:, w], w_inL[:, w], xh[:, :], xl[:, :]).then_inc(sem["b_xin"], 1)
                    if has(f) and i == 0:
                        if has(t):
                            pe.wait_ge(sem["b_gT"], t + 1)
                        for j in range(J):
                            ps = q_Q[:, j * NR:(j + 1) * NR]
                            mm(ps, xh[:, j::J], rwH[:, :], True, False)
                            mm(ps, xl[:, j::J], rwH[:, :], False, False)
                            last = mm(ps, xh[:, j::J], rwL[:, :], False, True)
                        last.then_inc(sem["b_rout"], 1)
                    if has(m):
                        after(pe, sem["b_actg"], RC * m)
                        for k in range(IC):
                            last = mm(q_D[i][:, :], wdel[:, k, i * P:(i + 1) * P], xc2[:, k, :], k == 0, k == IC - 1)
                        last.then_inc(sem["b_d"], 1)
                if has(t):
                    pe.wait_ge(sem["b_sg"], t + 1)
                    pe.wait_ge(sem["b_lg"], at_most(t + 3))
                    if not has(f):
                        pe.wait_ge(sem["b_gT"], t + 1)
                    turn_back(q_Q).then_inc(sem["b_sgT"], 1)
                if has(f):
                    for i in range(IC):
                        w = slice(DI + i * P, DI + (i + 1) * P)
                        split3((q_T, q_S)[i][:, :], w_inH[:, w], w_inL[:, w], xh[:, :], xl[:, :]).then_inc(sem["b_res"], 1)

                def spread(c):
                    if c < 2:
                        pe.wait_ge(sem["b_delta"], IC * m + c + 1)
                    else:
                        pe.wait_ge(sem["b_actg"], RC * m + c - 1)
                    mm(q_D[c % 2][:, :], sel[:, c, :], gT[:, :]).then_inc(sem["b_gate"], 1)

                def expert_in(c):
                    if c < 2:
                        pe.wait_ge(sem["b_u0"], IC * f + c + 1)
                    else:
                        pe.wait_ge(sem["b_act"], UC * f + c - 1)
                    w = slice(c * P, (c + 1) * P)
                    split3(q_U[c % 2][:, :], upH[:, w], upL[:, w], xh[:, :], xl[:, :]).then_inc(sem["b_up"], 1)

                if has(m):
                    pe.wait_ge(sem["b_g4"], m + 1)
                    if has(t):
                        pe.wait_ge(sem["b_out"], t + 1)
                    elif has(f):
                        pe.wait_ge(sem["b_lg"], f + 1)
                    after(pe, sem["b_gp"], m)
                    mm(q_F[:, :], dnT[:, 0, :], act[:, 0, :], True, False)
                    gps = q_Q[0:3 * NR, 0:N // 2].bitcast(BF16)
                    for j in range(J):
                        last = nc.tensor.transpose(gps[:, j * P:(j + 1) * P], g3[:, j, :, :].rearrange("p a r -> p (a r)"),
                                                   identb[:, :])
                    last.then_inc(sem["b_gtT"], 1)
                if has(f):
                    expert_in(0)
                if has(m):
                    pe.wait_ge(sem["b_gT"], m + 1)
                    spread(0)
                    spread(1)
                for c in range(RC):
                    if has(m):
                        pe.wait_ge(sem["b_actg"], RC * m + c + 1)
                        last = mm(q_F[:, :], dnT[:, c + 1, :], act[:, c + 1, :], False, c == RC - 1)
                        if c == RC - 1:
                            last.then_inc(sem["b_down"], 1)
                        if c + 2 < RC:
                            spread(c + 2)
                    if has(f):
                        expert_in(c + 1)
                    if has(m) and c == 1:
                        if has(f):
                            pe.wait_ge(sem["b_r2"], IC * f + 1)
                        for k in range(IC):
                            last = mm(q_T[:, :], wb[:, k, :], xc2[:, k, :], k == 0, k == IC - 1)
                        last.then_inc(sem["b_b"], 1)
                if has(m):
                    pe.wait_ge(sem["b_y"], IC * m + IC)
                    if has(f):
                        pe.wait_ge(sem["b_r2"], IC * f + IC)
                    elif has(t):
                        pe.wait_ge(sem["b_sg"], t + 1)
                    for k in range(IC):
                        last = mm(q_S[:, :], w_out[:, k, :], yb[:, k, :], k == 0, k == IC - 1)
                    last.then_inc(sem["b_s"], 1)

            pe.wait_ge(sem["a_x1"], G)
            pe.wait_ge(sem["prep_sbuf"], 1)
            pe.wait_ge(sem["ident_ready"], 2)
            pe.wait_ge(sem["sel_ready"], 4)
            bodies(pe, layer1)


_INS = ["L0_attn_x", "L0_attn_time_decay", "L0_attn_time_first", "L0_attn_time_mix", "L0_attn_Wk", "L0_attn_Wv",
        "L0_attn_Wr", "L0_attn_Wo", "L0_ffn_k0", "L0_ffn_k1", "L0_ffn_k2", "L0_ffn_s0", "L0_ffn_s1", "L0_ffn_s2",
        "L1_attn_W_in", "L1_attn_conv_w", "L1_attn_conv_b", "L1_attn_W_x", "L1_attn_W_dt", "L1_attn_b_dt",
        "L1_attn_W_out", "L1_ffn_shared_up", "L1_ffn_shared_down", "L1_ffn_routed_up", "L1_ffn_routed_down",
        "L1_ffn_router_w"]


def kernel(**inputs):
    import numpy as _np
    import concourse.bacc as _bacc
    from concourse import mybir as _mybir
    from concourse.bass_utils import run_bass_kernel_spmd as _run

    nc = _bacc.Bacc("TRN2", target_bir_lowering=False, num_devices=1)
    arrays, args = {}, {}
    for name in _INS:
        a = _np.ascontiguousarray(inputs[name])
        if a.ndim == 0:
            a = a.reshape(1)
        arrays[f"in_{name}"] = a
        args[name] = nc.dram_tensor(f"in_{name}", a.shape, _mybir.dt.from_np(a.dtype), kind="ExternalInput").ap()
    out = nc.dram_tensor("out_0", inputs["L0_attn_x"].shape, F32, kind="ExternalOutput").ap()
    build(nc, args, out)
    r = _run(nc, [arrays], core_ids=[0])
    return r.results[0]["out_0"]
```

```python
from contextlib import ExitStack
import math

import concourse.bass as bass
from concourse import mybir

ALU = mybir.AluOpType
ACT = mybir.ActivationFunctionType
AX = mybir.AxisListType
F32 = mybir.dt.float32
F16 = mybir.dt.float16
BF16 = mybir.dt.bfloat16
U8 = mybir.dt.uint8

P = 128
EPS = 1e-5
ARENA = 23 * 1024
WK_EPS = 1e-9
K_CAP = 60.0
SP_CAP = 30.0
XS = 2.0 ** 11
W0S = 2.0 ** -4
W1S = 2.0 ** -9
FS = 4.0 * 2.0 ** 2

SEM_NAMES = """
x_loaded wq_loaded wa_loaded wk_loaded wb_loaded ident_ready sel_ready const_ready signs_ready chan_ready chain mix_ready w1_ready const_done
square_turned square_ready absmax_ready absmax_all scales_ready prep_turned prep_high prep_out prep_sbuf
bn_done
a_stat a_vareps a_rstd a_centred a_xn a_xnT a_prev a_xh a_xm a_xl a_k a_v a_r a_ek a_ekm a_kv a_scanK a_scanV
a_wkc a_kvc a_wk a_wkv a_thr a_sr a_ysr a_rec a_y a_z0 a_z1 a_hi0 a_hi1 a_lo0 a_relu a_low a_lo1 a_s a_f a_thf a_gp a_sg a_sgT a_x1
b_stat b_vareps b_rstd b_centred b_xn b_xnT b_xh b_xl b_xin b_res b_rout b_u0 b_conv b_thu b_xc2 b_xch b_xcl b_thr b_r2
b_mx b_lg b_pe b_sum b_rs b_top b_fill b_rep b_gt b_gn b_g1 b_g2 b_g3 b_g4 b_gtT b_gT
b_up b_act b_high0 b_low0 b_actg b_high b_low b_gate b_down b_d b_xdt b_e b_em b_ln b_delta b_c b_cr b_b b_bx b_scan b_y b_s b_thf b_gp b_sg b_sgT b_out
stored
""".split()


def build(nc, A, out):
    B, T, C = A["L0_attn_x"].shape
    SEQ = 512 // T
    N = SEQ * T
    J = N // P
    G = B * T // N
    F = A["L0_ffn_k0"].shape[1]
    FC = F // P
    POOLED = 2
    DI = A["L1_attn_W_in"].shape[1] // 2
    IC = DI // P
    DS = A["L1_attn_W_dt"].shape[0]
    TAPS = A["L1_attn_conv_w"].shape[2]
    NR, E, _ = A["L1_ffn_routed_up"].shape
    NS = A["L1_ffn_shared_up"].shape[0]
    TOP_K = 4
    UC = (NS + NR) * E // P
    RC = NR * E // P
    RING = 4
    assert RC % RING == 0
    I_IN, I_UP, I_RW, I_WX, I_DT, I_DN, I_CW, I_CB = range(8)
    NSC = 8
    X_SC, X_IN, X_TANH, C_FAC, B_FAC, D_FAC, A_SC, F_FAC = range(8)

    x_d = A["L0_attn_x"].rearrange("b t c -> (b t) c").rearrange("(g p j) c -> g p (j c)", p=P, j=J)
    out_d = out.rearrange("b t c -> (b t) c").rearrange("(g p j) c -> g p (j c)", p=P, j=J)

    with ExitStack() as ctx:
        def sb(name, shape, dt=F32):
            return ctx.enter_context(nc.sbuf_tensor(name, shape, dt))

        sem = {n: ctx.enter_context(nc.semaphore(n)) for n in SEM_NAMES}

        bank = [ctx.enter_context(nc.psum_tensor(f"bank{i}", [P, 512], F32)) for i in range(8)]

        x_all = sb("x_all", [P, G * N])
        ident = sb("ident", [P, P])
        identb = sb("identb", [P, P], BF16)
        ones = sb("ones", [P, P])
        neghalf = sb("neghalf", [P, J])
        epsc = sb("epsc", [P, J])
        sel = sb("sel", [3 * NR, RC, P], BF16)

        wsq = sb("wsq", [P, 4, P])
        k0_u = sb("k0_u", [P, 2, F], U8)
        k1_u = sb("k1_u", [P, FC, F], U8)
        k2_u = sb("k2_u", [P, FC, P], U8)
        scal = sb("scal", [P, 3])
        chan = sb("chan", [P, 3])
        w_in = sb("w_in", [P, 2 * DI])
        cw = sb("cw", [P, IC, TAPS])
        cb = sb("cb", [P, IC])
        bdt = sb("bdt", [P, IC])
        wx = sb("wx", [P, IC, 2 * DS + DI])
        wdt = sb("wdt", [DS, DI])
        w_out = sb("w_out", [P, IC, P])
        up_n = sb("up_n", [P, UC, P])
        dn_n = sb("dn_n", [P, UC, P])
        rw_n = sb("rw_n", [NR, P])

        wsqT = sb("wsqT", [P, 4, P])
        w0 = sb("w0", [P, F], F16)
        w0d = sb("w0d", [P, F])
        w1 = sb("w1", [P, FC, F], F16)
        w2 = sb("w2", [P, FC, P], F16)
        sg_ = sb("sg_", [P, 2])
        sab = sb("sab", [P, 2])
        w0c = sb("w0c", [P, 1])
        w1c = sb("w1c", [P, 2])
        c3 = sb("c3", [P, 4])
        tch = sb("tch", [P, 4])
        dec = sb("dec", [P, T])
        upH = sb("upH", [P, UC * P], F16)
        upL = sb("upL", [P, UC * P], F16)
        rwH = sb("rwH", [P, NR], F16)
        rwL = sb("rwL", [P, NR], F16)
        w_inH = sb("w_inH", [P, 2 * DI], F16)
        w_inL = sb("w_inL", [P, 2 * DI], F16)
        amax = sb("amax", [P, NSC])
        pow2 = sb("pow2", [P, NSC])
        wsc = sb("wsc", [P, NSC])
        inv = sb("inv", [P, NSC])
        xinv = sb("xinv", [P, 3])
        bnd = sb("bnd", [P, 2])
        fac = sb("fac", [P, 8])
        cbs = sb("cbs", [P, IC])
        cwi = sb("cwi", [P, IC])
        dnH = sb("dnH", [P, UC * P], F16)
        dnL = sb("dnL", [P, UC * P], F16)
        wxsT = sb("wxsT", [DS, IC, P])
        wdH = sb("wdH", [P, IC, DI], F16)
        wdL = sb("wdL", [P, IC, DI], F16)
        wcH = sb("wcH", [P, IC, DI], F16)
        wcL = sb("wcL", [P, IC, DI], F16)
        wdp = sb("wdp", [P, IC * DI])
        wbs = sb("wbs", [P, IC])
        wb = sb("wb", [P, IC, P])
        wbH = sb("wbH", [P, IC, P], F16)
        wbL = sb("wbL", [P, IC, P], F16)

        st = sb("st", [P, J, 6])
        mv = sb("mv", [P, J, 2])
        ve = sb("ve", [P, J])
        rstd = sb("rstd", [P, J])
        xn = sb("xn", [P, J, P])
        xh = sb("xh", [P, N], F16)
        xl = sb("xl", [P, N], F16)
        thf = sb("thf", [P, N])
        gp = sb("gp", [P, N])
        sg = sb("sg", [P, N])
        prev = sb("prev", [P, SEQ, T])
        Pk = sb("Pk", [P, SEQ, T + 1])
        Pv = sb("Pv", [P, SEQ, T + 1])
        xi = sb("xi", [P, IC, SEQ, T + TAPS - 1])
        pe_ = sb("pe_", [P, J, NR + TOP_K])

        arena = sb("arena", [P, ARENA])
        used = {0: 0, 1: 0}

        def tile(layer, shape, dt=F32):
            size = math.prod(shape[1:]) * (2 if dt in (F16, BF16) else 4) // 4
            flat = arena[0:shape[0], used[layer]:used[layer] + size]
            used[layer] += size
            flat = flat if dt == F32 else flat.bitcast(dt)
            names = "abcd"[:len(shape) - 1]
            if len(names) == 1:
                return flat
            return flat.rearrange(f"p ({' '.join(names)}) -> p {' '.join(names)}", **dict(zip(names, shape[1:])))

        xm = tile(0, [P, N])
        ek = tile(0, [P, N])
        ekm = tile(0, [P, N])
        kv = tile(0, [P, N])
        wkc = tile(0, [P, N])
        kvc = tile(0, [P, N])
        wk = tile(0, [P, N])
        wkv = tile(0, [P, N])
        rec = tile(0, [P, N])
        thr = tile(0, [P, N])
        sr = tile(0, [P, N])
        ysr = tile(0, [P, N])
        ya = tile(0, [P, N])
        relu = tile(0, [P, POOLED, N])
        hh = tile(0, [P, 2, FC, N], F16)
        hl = tile(0, [P, 2, FC, N], F16)
        u = tile(1, [P, IC, N])
        thu = tile(1, [P, IC, N])
        xc2 = tile(1, [P, IC, N])
        xch = tile(1, [P, IC, N], F16)
        xcl = tile(1, [P, IC, N], F16)
        th2 = tile(1, [P, IC, N])
        r2 = tile(1, [P, IC, N])
        lg = tile(1, [P, J, NR])
        mx = tile(1, [P, J])
        sm = tile(1, [P, J])
        rs = tile(1, [P, J])
        top = tile(1, [P, J, 8])
        rep = tile(1, [P, J, NR + TOP_K])
        gt = tile(1, [P, J, NR])
        gn = tile(1, [P, J, NR])
        gr = tile(1, [P, J, NR])
        g3 = tile(1, [P, J, 3, NR], BF16)
        gT = tile(1, [3 * NR, N], BF16)
        act = tile(1, [P, UC, N])
        prod = tile(1, [P, RING, N])
        ph = tile(1, [P, RING, N], F16)
        pl = tile(1, [P, RING, N], F16)
        s0h = tile(1, [P, N], F16)
        s0l = tile(1, [P, N], F16)
        xdt = tile(1, [P, IC, N])
        e_ = tile(1, [P, IC, N])
        delta = tile(1, [P, IC, N])
        cr = tile(1, [P, IC, N])
        bx = tile(1, [P, IC, N])
        H = tile(1, [P, IC, N])
        yb = tile(1, [P, IC, N])

        loads_q = [(wsq[:, i, :], A["L0_attn_" + n]) for i, n in enumerate(("Wk", "Wv", "Wr", "Wo"))]
        loads_q.append((k0_u[:, :, :], A["L0_ffn_k0"].rearrange("(k p) f -> p k f", p=P)))
        loads_a = [
            (chan[:, 2:3], A["L0_attn_time_mix"].rearrange("a b c -> c (a b)")),
            (chan[:, 0:1], A["L0_attn_time_decay"]),
            (chan[:, 1:2], A["L0_attn_time_first"]),
        ]
        loads_a += [(scal[:, i:i + 1], A["L0_ffn_" + n].partition_broadcast(P)) for i, n in enumerate(("s0", "s1", "s2"))]
        loads_k = [
            (k1_u[:, :, :], A["L0_ffn_k1"].rearrange("(k p) f -> p k f", p=P)),
            (k2_u[:, :, :], A["L0_ffn_k2"].rearrange("(k p) f -> p k f", p=P)),
        ]
        loads_b = [
            (w_in[:, :], A["L1_attn_W_in"]),
            (cw[:, :, :], A["L1_attn_conv_w"].rearrange("(k p) a t -> p k (a t)", p=P)),
            (cb[:, :], A["L1_attn_conv_b"].rearrange("(k p) -> p k", p=P)),
            (bdt[:, :], A["L1_attn_b_dt"].rearrange("(k p) -> p k", p=P)),
            (wx[:, :, :], A["L1_attn_W_x"].rearrange("(k p) m -> p k m", p=P)),
            (wdt[:, :], A["L1_attn_W_dt"]),
            (w_out[:, :, :], A["L1_attn_W_out"].rearrange("(k p) m -> p k m", p=P)),
            (up_n[:, 0, :], A["L1_ffn_shared_up"].rearrange("s e h -> (s e) h")),
            (up_n[:, 1:UC, :], A["L1_ffn_routed_up"].rearrange("(k r) e h -> (r e) k h", r=P // E)),
            (dn_n[:, 0, :].rearrange("h (s e) -> h s e", e=E), A["L1_ffn_shared_down"].rearrange("s h e -> h s e")),
            (dn_n[:, 1:UC, :].rearrange("h k (r e) -> h (k r) e", e=E),
             A["L1_ffn_routed_down"].rearrange("r h e -> h r e")),
            (rw_n[:, :], A["L1_ffn_router_w"]),
        ]
        WQ_ALL, WA_ALL, WK_ALL, WB_ALL = (16 * len(w) for w in (loads_q, loads_a, loads_k, loads_b))

        up_b = [[(up_n[:, c, :], P) for c in range(b, min(b + 4, UC))] for b in range(0, UC, 4)]
        dn_b = [[(dn_n[:, c, :], P) for c in range(b, min(b + 4, UC))] for b in range(0, UC, 4)]
        up_b[-1].append((rw_n[:, :], NR))
        dn_b[-1] += [(wx[:, k, 0:DS], P) for k in range(IC)]
        batches = up_b + dn_b
        UB, NB = len(up_b), len(up_b) + len(dn_b)
        assert len(up_b[-1]) == 2 and len(dn_b[-1]) == 1 + IC

        b_T, b_K, b_V, b_RX, b_Z0, b_Z1, b_S, b_F = bank
        q_T, q_Q, _, _, _, _, q_S, q_F = bank
        q_D = (bank[2], bank[3])
        q_U = (bank[4], bank[5])
        b_Z = ((b_K, b_V, b_Z0, b_Z1), (b_Z0, b_Z1, b_Z0, b_Z1))

        block = ctx.enter_context(nc.Block())

        def after(eng, semaphore, value):
            if not (isinstance(value, int) and value <= 0):
                eng.wait_ge(semaphore, value)

        def has(n):
            return not isinstance(n, int) or 0 <= n < G

        def at_most(n):
            return min(n, G) if isinstance(n, int) else n

        def bodies(eng, body, between={}):
            def peeled(n):
                body(n)
                if n in between:
                    between[n]()
            for n in range(3):
                peeled(n)
            with eng.Fori(3, G - 1) as n:
                body(n)
            for n in range(G - 1, G + 2):
                peeled(n)

        def xs_of(n):
            return x_all[:, bass.ds(n * N, N)]

        def seqs(ap):
            return ap.rearrange("p (s t) -> p s t", s=SEQ)

        @block.sync
        def _(sp):
            sp.dma_start(xs_of(0), x_d[0]).then_inc(sem["x_loaded"], 16)
            for dst, src in loads_q:
                sp.dma_start(dst, src).then_inc(sem["wq_loaded"], 16)
            sp.wait_ge(sem["x_loaded"], 16)
            sp.dma_start(xs_of(1), x_d[1]).then_inc(sem["x_loaded"], 16)
            for dst, src in loads_b:
                sp.dma_start(dst, src, allow_slow_non_contiguous=dst.shape[1] == IC).then_inc(sem["wb_loaded"], 16)
            with sp.Fori(2, G) as n:
                sp.wait_ge(sem["x_loaded"], n * 16)
                sp.dma_start(xs_of(n), x_d[bass.ds(n, 1)].rearrange("g p f -> (g p) f")).then_inc(sem["x_loaded"], 16)
            with sp.Fori(0, G) as n:
                sp.wait_ge(sem["b_out"], n + 1)
                sp.dma_start(out_d[bass.ds(n, 1)].rearrange("g p f -> (g p) f"), xs_of(n)).then_inc(sem["stored"], 16)
            sp.wait_ge(sem["stored"], 16 * G)

        @block.gpsimd
        def _(pool):
            g = nc.gpsimd
            for dst, src in loads_k:
                pool.dma_start(dst, src).then_inc(sem["wk_loaded"], 16)
            g.memset(ident[:, :], 0.0).then_inc(sem["const_ready"], 1)
            pool.wait_ge(sem["const_ready"], 1)
            g.affine_select(out=ident[:, :], in_=ident[:, :], compare_op=ALU.not_equal, fill=1.0, base=0,
                            pattern=[[-1, P]], channel_multiplier=1).then_inc(sem["ident_ready"], 1)
            g.memset(epsc[:, :], EPS).then_inc(sem["const_ready"], 1)
            g.memset(neghalf[:, :], -0.5).then_inc(sem["const_ready"], 1)
            pool.wait_ge(sem["const_ready"], 3)

            def normalise_step(n, ph, step):
                if step == 0:
                    pool.wait_ge(sem[ph + "stat"], n + 1)
                    g.tensor_tensor(ve[:, :], mv[:, :, 1], epsc[:, :], ALU.add).then_inc(sem[ph + "vareps"], 1)
                    pool.wait_ge(sem[ph + "vareps"], n + 1)
                    g.tensor_tensor(rstd[:, :], ve[:, :], neghalf[:, :], ALU.pow).then_inc(sem[ph + "rstd"], 1)
                elif step == 1:
                    after(pool, sem[ph + "xnT"], n)
                    g.tensor_tensor(xn[:, :, :], xs_of(n).rearrange("p (j c) -> p j c", j=J),
                                    mv[:, :, 0:1].to_broadcast([P, J, P]), ALU.subtract).then_inc(sem[ph + "centred"], 1)
                else:
                    pool.wait_ge(sem[ph + "rstd"], n + 1)
                    pool.wait_ge(sem[ph + "centred"], n + 1)
                    g.tensor_tensor(xn[:, :, :], xn[:, :, :], rstd[:, :].unsqueeze(2).to_broadcast([P, J, P]),
                                    ALU.mult).then_inc(sem[ph + "xn"], 1)

            def normalise(n, ph):
                for step in range(3):
                    normalise_step(n, ph, step)

            normalise(0, "a_")
            g.memset(ones[:, :], 1.0).then_inc(sem["const_ready"], 1)
            g.memset(prev[:, :, 0:1], 0.0).then_inc(sem["const_ready"], 1)
            g.memset(Pk[:, :, 0:1], 0.0).then_inc(sem["const_ready"], 1)
            g.memset(Pv[:, :, 0:1], 0.0).then_inc(sem["const_ready"], 1)
            g.memset(amax[:, :], 0.0).then_inc(sem["const_ready"], 1)
            g.memset(xi[:, :, :, 0:TAPS - 1], 0.0).then_inc(sem["const_ready"], 1)
            g.memset(pe_[:, :, NR:], -1.0).then_inc(sem["const_ready"], 1)
            pool.wait_ge(sem["wk_loaded"], WK_ALL)
            pool.wait_ge(sem["w1_ready"], 1)
            g.tensor_scalar(w1[:, :, :], k1_u[:, :, :], w1c[:, 0:1], w1c[:, 1:2], ALU.mult, ALU.add)
            g.tensor_scalar(w2[:, :, :], k2_u[:, :, :], 2.0, -1.0, ALU.mult, ALU.add).then_inc(sem["w1_ready"], 1)

            def layer0(n):
                f, m = n, n - 1
                if has(m):
                    for j in range(POOLED):
                        pool.wait_ge(sem["a_hi1"], FC * m + j + 1)
                        g.tensor_tensor(hl[:, 1, j, :], relu[:, j, :], hh[:, 1, j, :], ALU.subtract).then_inc(sem["a_low"], 1)
                    pool.wait_ge(sem["a_rec"], m + 1)
                    pool.wait_ge(sem["a_ysr"], m + 1)
                    after(pool, sem["a_s"], m)
                    g.tensor_tensor(ya[:, :], ysr[:, :], rec[:, :], ALU.mult).then_inc(sem["a_y"], 1)
                if has(f) and has(f + 1):
                    normalise(f + 1, "a_")
                if has(f):
                    pool.wait_ge(sem["a_wkc"], f + 1)
                    pool.wait_ge(sem["a_scanK"], f + 1)
                    g.tensor_tensor(seqs(wk[:, :]), seqs(wkc[:, :]), Pk[:, :, 0:T], ALU.add).then_inc(sem["a_wk"], 1)
                    pool.wait_ge(sem["a_kvc"], f + 1)
                    pool.wait_ge(sem["a_scanV"], f + 1)
                    g.tensor_tensor(seqs(wkv[:, :]), seqs(kvc[:, :]), Pv[:, :, 0:T], ALU.add).then_inc(sem["a_wkv"], 1)
                    pool.wait_ge(sem["a_wkv"], f + 1)
                    pool.wait_ge(sem["a_sr"], f + 1)
                    g.tensor_tensor(ysr[:, :], wkv[:, :], sr[:, :], ALU.mult).then_inc(sem["a_ysr"], 1)

            def constants():
                pool.wait_ge(sem["absmax_ready"], NSC)
                g.partition_all_reduce(amax[:, :], amax[:, :], P, bass.bass_isa.ReduceOp.max).then_inc(sem["absmax_all"], 1)
                g.memset(sel[:, :, :], 0.0).then_inc(sem["sel_ready"], 1)
                for b in range(3):
                    pool.wait_ge(sem["sel_ready"], b + 1)
                    v = sel[:, :, :].rearrange("k c (h e) -> k c h e", e=E)
                    g.affine_select(out=v, in_=v, compare_op=ALU.not_equal, fill=1.0, base=-NR * b,
                                    pattern=[[-(P // E), RC], [-1, P // E], [0, E]],
                                    channel_multiplier=1).then_inc(sem["sel_ready"], 1)
                g.tensor_copy(identb[:, :], ident[:, :]).then_inc(sem["ident_ready"], 1)

            bodies(pool, layer0, {1: constants, G - 1: lambda: normalise(0, "b_")})

            def low_gated(n, c):
                pool.wait_ge(sem["b_high"], RC * n + c + 1)
                r = c % RING
                g.tensor_tensor(pl[:, r, :], prod[:, r, :], ph[:, r, :], ALU.subtract).then_inc(sem["b_low"], 1)

            def layer1(n):
                f, m = n, n - 1
                ahead = has(f) and has(f + 1)
                for c in range(RC):
                    if has(m):
                        low_gated(m, c)
                    if ahead and c < 3:
                        normalise_step(f + 1, "b_", c)
                    if has(m) and c >= RC - 2:
                        k = c - RC + 2
                        pool.wait_ge(sem["b_cr"], IC * m + k + 1)
                        pool.wait_ge(sem["b_scan"], IC * m + k + 1)
                        after(pool, sem["b_s"], m)
                        g.tensor_tensor(yb[:, k, :], H[:, k, :], cr[:, k, :], ALU.mult).then_inc(sem["b_y"], 1)
                if has(f):
                    for k in range(IC):
                        pool.wait_ge(sem["b_xch"], IC * f + k + 1)
                        g.tensor_tensor(xcl[:, k, :], xc2[:, k, :], xch[:, k, :], ALU.subtract).then_inc(sem["b_xcl"], 1)

            bodies(pool, layer1)

        @block.scalar
        def _(actv):
            a = nc.scalar
            for dst, src in loads_a:
                actv.dma_start(dst, src).then_inc(sem["wa_loaded"], 16)
            actv.wait_ge(sem["wa_loaded"], WA_ALL)
            a.activation(sg_[:, :], scal[:, 0:2], ACT.Sign).then_inc(sem["signs_ready"], 1)
            a.activation(tch[:, 0:1], chan[:, 0:1], ACT.Exp).then_inc(sem["chan_ready"], 1)
            actv.wait_ge(sem["chan_ready"], 1)
            a.activation(tch[:, 1:2], tch[:, 0:1], ACT.Exp, scale=-1.0).then_inc(sem["chan_ready"], 1)
            a.activation(tch[:, 2:3], chan[:, 1:2], ACT.Exp).then_inc(sem["chan_ready"], 1)
            actv.wait_ge(sem["mix_ready"], 1)

            def high(layer, n, j):
                actv.wait_ge(sem[("a_z0", "a_z1")[layer]], FC * n + j + 1)
                if layer:
                    after(actv, sem["a_f"], n)
                src = b_Z[layer][j][:, :]
                if layer and j < POOLED:
                    after(actv, sem["a_low"], POOLED * n)
                    a.activation(relu[:, j, :], src, ACT.Relu).then_inc(sem["a_relu"], 1)
                    actv.wait_ge(sem["a_relu"], POOLED * n + j + 1)
                    src = relu[:, j, :]
                a.activation(hh[:, layer, j, :], src, ACT.Relu).then_inc(sem[("a_hi0", "a_hi1")[layer]], 1)

            def layer0(n):
                f, m = n, n - 1
                if has(f):
                    actv.wait_ge(sem["a_xnT"], f + 1)
                    after(actv, sem["a_xm"], f)
                    a.activation(prev[:, :, 1:T], seqs(b_T[:, :])[:, :, 0:T - 1], ACT.Copy,
                                 scale=tch[:, 3:4]).then_inc(sem["a_prev"], 1)
                    after(actv, sem["a_z0"], FC * f)
                    a.activation(xh[:, :], b_T[:, :], ACT.Copy, scale=XS).then_inc(sem["a_xh"], 1)
                if has(m):
                    high(1, m, 0)
                    high(1, m, 1)
                if has(f):
                    actv.wait_ge(sem["a_k"], f + 1)
                    after(actv, sem["a_ekm"], f)
                    a.activation(ek[:, :], b_K[:, :], ACT.Exp).then_inc(sem["a_ek"], 1)
                if has(m):
                    high(1, m, 2)
                if has(f):
                    actv.wait_ge(sem["a_ekm"], f + 1)
                    after(actv, sem["a_wk"], f)
                    a.activation(wkc[:, :], ekm[:, :], ACT.Copy, scale=tch[:, 2:3], bias=WK_EPS).then_inc(sem["a_wkc"], 1)
                if has(m):
                    high(1, m, 3)
                if has(f):
                    actv.wait_ge(sem["a_kv"], f + 1)
                    after(actv, sem["a_wkv"], f)
                    a.activation(kvc[:, :], kv[:, :], ACT.Copy, scale=tch[:, 2:3]).then_inc(sem["a_kvc"], 1)
                    actv.wait_ge(sem["a_r"], f + 1)
                    a.activation(thr[:, :], b_RX[:, :], ACT.Tanh, scale=0.5).then_inc(sem["a_thr"], 1)
                    high(0, f, 0)
                    actv.wait_ge(sem["a_thr"], f + 1)
                    after(actv, sem["a_ysr"], f)
                    a.activation(sr[:, :], thr[:, :], ACT.Copy, scale=0.5, bias=0.5).then_inc(sem["a_sr"], 1)
                    high(0, f, 1)
                    high(0, f, 2)
                    high(0, f, 3)
                if has(m):
                    actv.wait_ge(sem["a_f"], m + 1)
                    after(actv, sem["a_gp"], m)
                    if isinstance(m, int) and m == 0:
                        actv.wait_ge(sem["const_done"], 1)
                    a.activation(thf[:, :], b_F[:, :], ACT.Tanh, scale=c3[:, 2:3]).then_inc(sem["a_thf"], 1)
            def weights():
                turned_high(0)
                actv.wait_ge(sem["scales_ready"], 1)
                for i in range(NB):
                    actv.wait_ge(sem["prep_turned"], i + 1)
                    to, sc, b = (upH, I_UP, i) if i < UB else (dnH, I_DN, i - UB)
                    w = min(UC * P - 4 * b * P, 4 * P)
                    last = a.activation(to[:, 4 * b * P:4 * b * P + w], (b_K, b_V)[i % 2][:, 0:w], ACT.Copy,
                                        scale=wsc[:, sc:sc + 1])
                    if i == UB - 1:
                        last = a.activation(rwH[:, :], (b_K, b_V)[i % 2][:, w:w + NR], ACT.Copy, scale=wsc[:, I_RW:I_RW + 1])
                    last.then_inc(sem["prep_high"], 1)
            def turned_high(n):
                actv.wait_ge(sem["b_xnT"], n + 1)
                after(actv, sem["b_up"], UC * n)
                a.activation(xh[:, :], q_T[:, :], ACT.Copy, scale=XS).then_inc(sem["b_xh"], 1)

            bodies(actv, layer0, {G: weights})

            GELU_SET, EXP_SET = "gelu_and_others", "natural_log_exp_and_others"

            def layer1(n):
                f, m, t = n, n - 1, n - 2

                def step_size(k):
                    actv.wait_ge(sem["b_d"], IC * m + k + 1)
                    after(actv, sem["b_delta"], IC * m)
                    a.activation(xdt[:, k, :], (q_T, q_S)[k][:, :], ACT.Identity, scale=fac[:, D_FAC:D_FAC + 1],
                                 bias=bdt[:, k:k + 1]).then_inc(sem["b_xdt"], 1)

                def exponential(k):
                    actv.wait_ge(sem["b_xdt"], IC * m + k + 1)
                    a.activation(e_[:, k, :], xdt[:, k, :], ACT.Exp).then_inc(sem["b_e"], 1)

                def logarithm(k):
                    actv.wait_ge(sem["b_em"], IC * m + k + 1)
                    a.activation(e_[:, k, :], e_[:, k, :], ACT.Ln, bias=1.0).then_inc(sem["b_ln"], 1)

                def conv_input(k):
                    actv.wait_ge(sem["b_xin"], IC * f + k + 1)
                    after(actv, sem["b_conv"], IC * f * (TAPS - 1))
                    after(actv, sem["b_xc2"], IC * f)
                    a.activation(xi[:, k, :, TAPS - 1:], seqs(q_U[k][:, :]), ACT.Copy, scale=fac[:, X_IN:X_IN + 1])
                    a.activation(u[:, k, :], q_U[k][:, :], ACT.Identity, scale=cwi[:, k:k + 1],
                                 bias=cbs[:, k:k + 1]).then_inc(sem["b_u0"], 1)

                def res_tanh(k):
                    actv.wait_ge(sem["b_res"], IC * f + k + 1)
                    after(actv, sem["b_r2"], IC * f)
                    a.activation(th2[:, k, :], (q_T, q_S)[k][:, :], ACT.Tanh,
                                 scale=fac[:, X_TANH:X_TANH + 1]).then_inc(sem["b_thr"], 1)

                def half_tanh(k):
                    actv.wait_ge(sem["b_conv"], (IC * f + k + 1) * (TAPS - 1))
                    a.activation(thu[:, k, :], u[:, k, :], ACT.Tanh, scale=fac[:, X_SC:X_SC + 1]).then_inc(sem["b_thu"], 1)

                def high_xc(k):
                    actv.wait_ge(sem["b_xc2"], IC * f + k + 1)
                    after(actv, sem["b_b"], f)
                    a.activation(xch[:, k, :], xc2[:, k, :], ACT.Copy).then_inc(sem["b_xch"], 1)

                def high_gated(c):
                    actv.wait_ge(sem["b_actg"], RC * m + c + 1)
                    after(actv, sem["b_down"], UC * m + c + 2 - RING if c >= RING else UC * m)
                    a.activation(ph[:, c % RING, :], prod[:, c % RING, :], ACT.Copy).then_inc(sem["b_high"], 1)

                def gelu(c):
                    actv.wait_ge(sem["b_up"], UC * f + c + 1)
                    if has(m):
                        if c:
                            actv.wait_ge(sem["b_actg"], RC * m + c)
                        else:
                            actv.wait_ge(sem["b_low0"], m + 1)
                    a.activation(act[:, c, :], q_U[c % 2][:, :], ACT.Gelu, scale=xinv[:, I_UP:I_UP + 1]).then_inc(sem["b_act"], 1)

                if has(m):
                    actv.wait_ge(sem["b_act"], UC * m + 1)
                    after(actv, sem["b_down"], UC * m)
                    a.activation(s0h[:, :], act[:, 0, :], ACT.Copy, scale=fac[:, A_SC:A_SC + 1]).then_inc(sem["b_high0"], 1)
                if has(t):
                    actv.wait_ge(sem["b_down"], UC * (t + 1))
                    after(actv, sem["b_gp"], t)
                    a.activation(thf[:, :], q_F[:, :], ACT.Tanh, scale=fac[:, F_FAC:F_FAC + 1]).then_inc(sem["b_thf"], 1)
                if has(m):
                    actv.wait_ge(sem["b_gtT"], m + 1)
                    after(actv, sem["b_gate"], RC * m)
                    a.copy(gT[:, :].rearrange("r (p j) -> r j p", j=J),
                           q_Q[0:3 * NR, 0:N // 2].bitcast(BF16).rearrange("r (j p) -> r j p", j=J)).then_inc(sem["b_gT"], 1)
                a.preload_act_table_set(EXP_SET)
                if has(f):
                    conv_input(0)
                if has(m):
                    step_size(0)
                    exponential(0)
                    high_gated(0)
                if has(f):
                    conv_input(1)
                if has(m):
                    high_gated(1)
                    step_size(1)
                    exponential(1)
                if has(f):
                    actv.wait_ge(sem["b_lg"], f + 1)
                    after(actv, sem["b_gt"], f)
                    a.activation(pe_[:, :, 0:NR], lg[:, :, :], ACT.Exp, scale=xinv[:, I_RW:I_RW + 1]).then_inc(sem["b_pe"], 1)
                if has(m):
                    logarithm(0)
                    logarithm(1)
                    high_gated(2)
                a.preload_act_table_set(GELU_SET)
                if has(f):
                    half_tanh(0)
                    res_tanh(0)
                if has(m):
                    high_gated(3)
                if has(f):
                    half_tanh(1)
                    res_tanh(1)
                if has(m):
                    high_gated(4)
                for c in range(UC):
                    if has(f):
                        gelu(c)
                    if has(m) and c < 3:
                        high_gated(c + 5)
                    if has(f) and c in (4, 5):
                        high_xc(c - 4)
                if has(f) and has(f + 1):
                    turned_high(f + 1)

            bodies(actv, layer1)

        @block.vector
        def _(dve):
            v = nc.vector
            steps = [0]

            def link(ins):
                steps[0] += 1
                ins.then_inc(sem["chain"], 1)
                dve.wait_ge(sem["chain"], steps[0])

            def row_stats(n):
                for j in range(J):
                    last = v.bn_stats(st[:, j, :], x_all[:, bass.ds(n * N + j * P, P)])
                last.then_inc(sem["bn_done"], 1)

            def row_moments(ready):
                for j in range(J):
                    last = v.bn_aggr(mv[:, j, :], st[:, j, :])
                last.then_inc(ready, 1)

            dve.wait_ge(sem["x_loaded"], 16)
            row_stats(0)
            dve.wait_ge(sem["bn_done"], 1)
            row_moments(sem["a_stat"])
            def links(*instructions):
                for ins in instructions:
                    steps[0] += 1
                    ins.then_inc(sem["chain"], 1)
                dve.wait_ge(sem["chain"], steps[0])

            dve.wait_ge(sem["wa_loaded"], WA_ALL)
            v.tensor_scalar(tch[:, 3:4], chan[:, 2:3], -1.0, 1.0, ALU.mult, ALU.add).then_inc(sem["mix_ready"], 1)
            dve.wait_ge(sem["signs_ready"], 1)
            v.tensor_scalar(w1c[:, 0:1], sg_[:, 1:2], 2.0 * W1S, None, ALU.mult)
            v.tensor_scalar(w1c[:, 1:2], sg_[:, 1:2], -W1S, None, ALU.mult).then_inc(sem["w1_ready"], 1)
            dve.wait_ge(sem["wq_loaded"], WQ_ALL)
            links(v.tensor_scalar(w0c[:, :], sg_[:, 0:1], 2.0 * W0S, None, ALU.mult),
                  v.tensor_tensor(w0d[:, :], k0_u[:, 0, :], k0_u[:, 1, :], ALU.subtract),
                  v.tensor_tensor(sab[:, :], scal[:, 0:2], sg_[:, :], ALU.mult))
            links(v.tensor_scalar(w0[:, :], w0d[:, :], w0c[:, 0:1], None, ALU.mult),
                  v.tensor_tensor(c3[:, 0:1], sab[:, 0:1], sab[:, 1:2], ALU.mult))
            dve.wait_ge(sem["square_turned"], 1)
            v.tensor_copy(wsqT[:, :, :].rearrange("p a b -> p (a b)"), b_S[:, :]).then_inc(sem["square_ready"], 1)
            dve.wait_ge(sem["const_ready"], 7)
            dve.wait_ge(sem["chan_ready"], 3)
            links(v.scalar_tensor_tensor(c3[:, 1:2], c3[:, 0:1], FS, scal[:, 2:3], ALU.mult, ALU.mult),
                  v.tensor_scalar(dec[:, 0:P], ones[:, :], tch[:, 1:2], None, ALU.mult),
                  v.tensor_scalar(dec[:, P:T], ones[:, 0:T - P], tch[:, 1:2], None, ALU.mult))
            v.tensor_scalar(c3[:, 2:3], c3[:, 1:2], 0.5, None, ALU.mult).then_inc(sem["const_done"], 1)

            def low(layer, n, j):
                dve.wait_ge(sem[("a_hi0", "a_hi1")[layer]], FC * n + j + 1)
                v.scalar_tensor_tensor(hl[:, layer, j, :], b_Z[layer][j][:, :], 0.0, hh[:, layer, j, :],
                                       ALU.max, ALU.subtract).then_inc(sem[("a_lo0", "a_lo1")[layer]], 1)

            def layer0(n):
                f, m, t = n, n - 1, n - 2
                ahead = has(f) and has(f + 1)
                if has(f):
                    dve.wait_ge(sem["a_xh"], f + 1)
                    after(dve, sem["a_r"], f)
                    v.scalar_tensor_tensor(xm[:, :], b_T[:, :], chan[:, 2:3], prev[:, :, :].rearrange("p s t -> p (s t)"),
                                           ALU.mult, ALU.add).then_inc(sem["a_xm"], 1)
                    if ahead:
                        dve.wait_ge(sem["x_loaded"], f * 16 + 32)
                        row_stats(f + 1)
                        dve.wait_ge(sem["a_xn"], f + 1)
                        dve.wait_ge(sem["bn_done"], f + 2)
                    after(dve, sem["a_z0"], FC * f)
                    v.scalar_tensor_tensor(xl[:, :], b_T[:, :], XS, xh[:, :], ALU.mult, ALU.subtract).then_inc(sem["a_xl"], 1)
                    if ahead:
                        row_moments(sem["a_stat"])
                if has(m):
                    dve.wait_ge(sem["a_wk"], m + 1)
                    after(dve, sem["a_y"], m)
                    v.reciprocal(rec[:, 0:N // 2], wk[:, 0:N // 2])
                if has(t):
                    dve.wait_ge(sem["a_sgT"], t + 1)
                    v.tensor_tensor(xs_of(t), xs_of(t), b_RX[:, :], ALU.add).then_inc(sem["a_x1"], 1)
                if has(f):
                    dve.wait_ge(sem["a_ek"], f + 1)
                    after(dve, sem["a_wkc"], f)
                    v.tensor_scalar(ekm[:, :], ek[:, :], math.exp(K_CAP), None, ALU.min).then_inc(sem["a_ekm"], 1)
                    dve.wait_ge(sem["a_ekm"], f + 1)
                    dve.wait_ge(sem["a_v"], f + 1)
                    after(dve, sem["a_kvc"], f)
                    v.tensor_tensor(kv[:, :], ekm[:, :], b_V[:, :], ALU.mult).then_inc(sem["a_kv"], 1)
                if has(m):
                    v.reciprocal(rec[:, N // 2:], wk[:, N // 2:]).then_inc(sem["a_rec"], 1)
                    low(1, m, 2)
                    low(1, m, 3)
                if has(f):
                    after(dve, sem["a_wk"], f)
                    for s in range(SEQ):
                        last = v.tensor_tensor_scan(Pk[:, s, 1:], dec[:, :], ekm[:, s * T:(s + 1) * T], 0.0,
                                                    ALU.mult, ALU.add)
                    last.then_inc(sem["a_scanK"], 1)
                if has(f):
                    dve.wait_ge(sem["a_kv"], f + 1)
                    after(dve, sem["a_wkv"], f)
                    for s in range(SEQ):
                        last = v.tensor_tensor_scan(Pv[:, s, 1:], dec[:, :], kv[:, s * T:(s + 1) * T], 0.0,
                                                    ALU.mult, ALU.add)
                    last.then_inc(sem["a_scanV"], 1)
                    low(0, f, 0)
                    low(0, f, 1)
                if has(f):
                    low(0, f, 2)
                    low(0, f, 3)
                if has(m):
                    dve.wait_ge(sem["a_thf"], m + 1)
                    after(dve, sem["a_sg"], m)
                    v.scalar_tensor_tensor(gp[:, :], thf[:, :], 1.0, b_F[:, :], ALU.add, ALU.mult).then_inc(sem["a_gp"], 1)
                    dve.wait_ge(sem["a_gp"], m + 1)
                    dve.wait_ge(sem["a_s"], m + 1)
                    after(dve, sem["a_sgT"], m)
                    v.scalar_tensor_tensor(sg[:, :], b_S[:, :], c3[:, 2:3], gp[:, :], ALU.mult, ALU.mult).then_inc(sem["a_sg"], 1)

            def magnitudes():
                flat = "p a b -> p (a b)"
                dve.wait_ge(sem["wb_loaded"], WB_ALL)
                dve.wait_ge(sem["const_ready"], 10)
                for i, w in ((I_IN, w_in[:, :]), (I_UP, up_n[:, :, :].rearrange(flat)), (I_RW, rw_n[:, :]),
                             (I_WX, wx[:, :, :].rearrange(flat)), (I_DT, wdt[:, :]), (I_DN, dn_n[:, :, :].rearrange(flat)),
                             (I_CW, cw[:, :, :].rearrange(flat)), (I_CB, cb[:, :])):
                    v.tensor_reduce(amax[0:w.shape[0], i:i + 1], w, AX.X, ALU.max,
                                    apply_absolute_value=True).then_inc(sem["absmax_ready"], 1)

            def col(t, i):
                return t[:, i:i + 1]

            def scales():
                flat = "p a b -> p (a b)"
                dve.wait_ge(sem["absmax_all"], 1)

                def pow2_of(dst, src):
                    return v.tensor_scalar(dst.bitcast(mybir.dt.int32), src.bitcast(mybir.dt.int32), 0x7F800000,
                                           None, ALU.bitwise_and)

                links(v.scalar_tensor_tensor(col(bnd, 0), col(amax, I_CW), float(TAPS * P), col(amax, I_IN), ALU.mult, ALU.mult),
                      v.tensor_reduce(wbs[:, :], wx[:, :, DS:2 * DS], AX.X, ALU.add))
                links(v.tensor_tensor(col(bnd, 0), col(bnd, 0), col(amax, I_CB), ALU.add),
                      v.tensor_scalar(pow2[:, :], amax[:, :], 1e-12, None, ALU.max))
                links(v.tensor_scalar(col(bnd, 0), col(bnd, 0), 1e-12, None, ALU.max), pow2_of(pow2[:, :], pow2[:, :]))
                links(pow2_of(col(bnd, 1), col(bnd, 0)),
                      v.tensor_scalar(inv[:, :], pow2[:, :], 2.0 ** -13, None, ALU.mult))
                links(v.tensor_scalar(col(fac, X_SC), col(bnd, 1), 2.0 ** -14, None, ALU.mult),
                      v.tensor_scalar(col(bnd, 1), col(bnd, 1), 2.0 ** -13, None, ALU.mult),
                      v.reciprocal(wsc[:, :], inv[:, :]),
                      v.tensor_scalar(xinv[:, :], inv[:, 0:3], 1.0 / XS, None, ALU.mult))
                links(v.tensor_scalar(col(fac, A_SC), col(wsc, I_UP), 2.0 ** (15 - 13) / (2 * P), None, ALU.mult),
                      v.reciprocal(col(bnd, 0), col(bnd, 1)),
                      v.tensor_scalar(col(fac, X_TANH), col(xinv, I_IN), 0.5, None, ALU.mult),
                      v.scalar_tensor_tensor(col(fac, C_FAC), col(inv, I_WX), 0.25, col(bnd, 1), ALU.mult, ALU.mult),
                      v.scalar_tensor_tensor(col(fac, B_FAC), col(inv, I_WX), 0.25 * DS, col(bnd, 1), ALU.mult, ALU.mult),
                      v.scalar_tensor_tensor(col(fac, D_FAC), col(inv, I_WX), 0.5 * DS * 2.0 ** 14, col(inv, I_DT),
                                             ALU.mult, ALU.mult))
                links(v.tensor_tensor(col(fac, X_IN), col(xinv, I_IN), col(bnd, 0), ALU.mult),
                      v.tensor_scalar(cbs[:, :], cb[:, :], col(bnd, 0), None, ALU.mult),
                      v.tensor_tensor(col(fac, C_FAC), col(fac, C_FAC), col(xinv, I_IN), ALU.mult),
                      v.tensor_tensor(col(fac, B_FAC), col(fac, B_FAC), col(bnd, 1), ALU.mult),
                      v.tensor_tensor(col(fac, D_FAC), col(fac, D_FAC), col(bnd, 1), ALU.mult),
                      v.reciprocal(col(fac, F_FAC), col(fac, A_SC)))
                v.tensor_scalar(cwi[:, :], cw[:, :, TAPS - 1], col(fac, X_IN), None, ALU.mult)
                v.scalar_tensor_tensor(col(fac, F_FAC), col(fac, F_FAC), 0.5, col(inv, I_DN), ALU.mult,
                                       ALU.mult).then_inc(sem["scales_ready"], 1)

            def matrices():
                flat = "p a b -> p (a b)"
                dve.wait_ge(sem["scales_ready"], 1)
                dve.wait_ge(sem["a_xn"], G)
                row_stats(0)
                dve.wait_ge(sem["bn_done"], G + 1)
                row_moments(sem["b_stat"])

                def halves(high, low, src, factor):
                    link(v.tensor_scalar(high, src, factor, None, ALU.mult))
                    return v.scalar_tensor_tensor(low, src, factor, high, ALU.mult, ALU.subtract)

                halves(w_inH[:, :], w_inL[:, :], w_in[:, :], col(wsc, I_IN))
                halves(wcH[:, :, :], wcL[:, :, :], wx[:, :, 2 * DS:], col(wsc, I_WX))
                for k in range(IC):
                    v.tensor_scalar(wb[:, k, :], ones[:, :], wbs[:, k:k + 1], 1.0 / DS, ALU.mult,
                                    ALU.mult).then_inc(sem["chain"], 1)
                    steps[0] += 1
                dve.wait_ge(sem["chain"], steps[0])
                halves(wbH[:, :, :], wbL[:, :, :], wb[:, :, :], col(wsc, I_WX))
                dve.wait_ge(sem["sel_ready"], 4)
                v.tensor_scalar(sel[:, :, :], sel[:, :, :], fac[0:3 * NR, A_SC:A_SC + 1], None,
                                ALU.mult).then_inc(sem["prep_sbuf"], 1)

            def turned_matrices():
                flat = "p a b -> p (a b)"
                turned_low(0)
                for i in range(NB + 1):
                    ps = (b_K, b_V)[i % 2]
                    if i < NB:
                        low, high, sc, b = (upL, upH, I_UP, i) if i < UB else (dnL, dnH, I_DN, i - UB)
                        w = min(UC * P - 4 * b * P, 4 * P)
                        part = slice(4 * b * P, 4 * b * P + w)
                        dve.wait_ge(sem["prep_high"], i + 1)
                        last = v.scalar_tensor_tensor(low[:, part], ps[:, 0:w], col(wsc, sc), high[:, part], ALU.mult, ALU.subtract)
                        if i == UB - 1:
                            last = v.scalar_tensor_tensor(rwL[:, :], ps[:, w:w + NR], col(wsc, I_RW), rwH[:, :],
                                                          ALU.mult, ALU.subtract)
                        if i == NB - 1:
                            last = v.tensor_scalar(wxsT[:, :, :].rearrange(flat), ps[0:DS, w:w + IC * P],
                                                   wsc[0:DS, I_WX:I_WX + 1], None, ALU.mult)
                    else:
                        dve.wait_ge(sem["prep_turned"], i + 1)
                        link(v.tensor_scalar(wdp[:, :], ps[:, 0:IC * DI], col(wsc, I_DT), 2.0 ** -14 / DS, ALU.mult, ALU.mult))
                        link(v.tensor_copy(wdH[:, :, :].rearrange(flat), wdp[:, :]))
                        last = v.tensor_tensor(wdL[:, :, :].rearrange(flat), wdp[:, :], wdH[:, :, :].rearrange(flat), ALU.subtract)
                    last.then_inc(sem["prep_out"], 1)

            def turned_low(n):
                dve.wait_ge(sem["b_xh"], n + 1)
                after(dve, sem["b_up"], UC * n)
                v.scalar_tensor_tensor(xl[:, :], q_T[:, :], XS, xh[:, :], ALU.mult, ALU.subtract).then_inc(sem["b_xl"], 1)

            bodies(dve, layer0, {0: magnitudes, 2: scales, G - 1: matrices, G: turned_matrices})

            def top_four(n):
                dve.wait_ge(sem["b_pe"], n + 1)
                v.reduce_sum(sm[:, :], pe_[:, :, 0:NR], AX.X).then_inc(sem["b_sum"], 1)
                for j in range(J):
                    last = v.max(top[:, j, :], pe_[:, j, 0:NR])
                last.then_inc(sem["b_top"], 1)
                dve.wait_ge(sem["b_top"], n + 1)
                v.memset(top[:, :, TOP_K:], -1.0).then_inc(sem["b_fill"], 1)
                dve.wait_ge(sem["b_sum"], n + 1)
                dve.wait_ge(sem["b_fill"], n + 1)
                v.reciprocal(rs[:, :], sm[:, :]).then_inc(sem["b_rs"], 1)
                for j in range(J):
                    last = v.match_replace(rep[:, j, :], top[:, j, :], pe_[:, j, :], 0.0)
                last.then_inc(sem["b_rep"], 1)

            def gates(n):
                dve.wait_ge(sem["b_rep"], n + 1)
                v.tensor_tensor(gt[:, :, :], pe_[:, :, 0:NR], rep[:, :, 0:NR], ALU.subtract).then_inc(sem["b_gt"], 1)
                dve.wait_ge(sem["b_gt"], n + 1)
                dve.wait_ge(sem["b_rs"], n + 1)
                v.tensor_tensor(gn[:, :, :], gt[:, :, :], rs[:, :].unsqueeze(2).to_broadcast([P, J, NR]),
                                ALU.mult).then_inc(sem["b_gn"], 1)
                dve.wait_ge(sem["b_gn"], n + 1)
                after(dve, sem["b_gtT"], n)
                v.tensor_copy(g3[:, :, 0, :], gn[:, :, :]).then_inc(sem["b_g1"], 1)
                dve.wait_ge(sem["b_g1"], n + 1)
                v.tensor_tensor(gr[:, :, :], gn[:, :, :], g3[:, :, 0, :], ALU.subtract).then_inc(sem["b_g2"], 1)
                dve.wait_ge(sem["b_g2"], n + 1)
                v.tensor_copy(g3[:, :, 1, :], gr[:, :, :]).then_inc(sem["b_g3"], 1)
                dve.wait_ge(sem["b_g3"], n + 1)
                v.tensor_tensor(g3[:, :, 2, :], gr[:, :, :], g3[:, :, 1, :], ALU.subtract).then_inc(sem["b_g4"], 1)

            def conv(n, k, t):
                i = (IC * n + k) * (TAPS - 1) + t
                if t == 0:
                    dve.wait_ge(sem["b_u0"], IC * n + k + 1)
                else:
                    dve.wait_ge(sem["b_conv"], i)
                uk = seqs(u[:, k, :])
                v.scalar_tensor_tensor(uk, xi[:, k, :, t:t + T], cw[:, k, t:t + 1], uk, ALU.mult, ALU.add)\
                    .then_inc(sem["b_conv"], 1)

            def layer1(n):
                f, m, t = n, n - 1, n - 2
                ahead = has(f) and has(f + 1)

                def gated(c):
                    dve.wait_ge(sem["b_act"], UC * m + c + 2)
                    after(dve, sem["b_low"], RC * m + c + 1 - RING if c >= RING else RC * m)
                    dve.wait_ge(sem["b_gate"], RC * m + c + 1)
                    v.tensor_tensor(prod[:, c % RING, :], act[:, c + 1, :], q_D[c % 2][:, :],
                                    ALU.mult).then_inc(sem["b_actg"], 1)

                def cap(k):
                    dve.wait_ge(sem["b_e"], IC * m + k + 1)
                    v.tensor_scalar(e_[:, k, :], e_[:, k, :], math.exp(SP_CAP), None, ALU.min).then_inc(sem["b_em"], 1)

                def softplus(k):
                    dve.wait_ge(sem["b_ln"], IC * m + k + 1)
                    v.tensor_tensor(delta[:, k, :], xdt[:, k, :], e_[:, k, :], ALU.max).then_inc(sem["b_delta"], 1)

                def output_weight(k):
                    dve.wait_ge(sem["b_c"], IC * m + k + 1)
                    after(dve, sem["b_y"], IC * m)
                    v.scalar_tensor_tensor(cr[:, k, :], q_U[k][:, :], fac[:, C_FAC:C_FAC + 1], r2[:, k, :],
                                           ALU.mult, ALU.mult).then_inc(sem["b_cr"], 1)

                def residual(k):
                    dve.wait_ge(sem["b_thr"], IC * f + k + 1)
                    after(dve, sem["b_cr"], IC * f)
                    v.scalar_tensor_tensor(r2[:, k, :], th2[:, k, :], 1.0, (q_T, q_S)[k][:, :], ALU.add,
                                           ALU.mult).then_inc(sem["b_r2"], 1)

                def state(k):
                    dve.wait_ge(sem["b_bx"], IC * m + k + 1)
                    dve.wait_ge(sem["b_delta"], IC * m + k + 1)
                    after(dve, sem["b_y"], IC * m)
                    for s in range(SEQ):
                        w = slice(s * T, (s + 1) * T)
                        last = v.tensor_tensor_scan(H[:, k, w], delta[:, k, w], bx[:, k, w], 0.0, ALU.mult, ALU.add)
                    last.then_inc(sem["b_scan"], 1)

                def activated(k):
                    dve.wait_ge(sem["b_thu"], IC * f + k + 1)
                    after(dve, sem["b_xcl"], IC * f)
                    after(dve, sem["b_bx"], IC * f)
                    v.scalar_tensor_tensor(xc2[:, k, :], thu[:, k, :], 1.0, u[:, k, :], ALU.add,
                                           ALU.mult).then_inc(sem["b_xc2"], 1)

                if has(m):
                    dve.wait_ge(sem["b_high0"], m + 1)
                    v.scalar_tensor_tensor(s0l[:, :], act[:, 0, :], fac[:, A_SC:A_SC + 1], s0h[:, :], ALU.mult,
                                           ALU.subtract).then_inc(sem["b_low0"], 1)
                if has(t):
                    dve.wait_ge(sem["b_thf"], t + 1)
                    v.scalar_tensor_tensor(gp[:, :], thf[:, :], 1.0, q_F[:, :], ALU.add, ALU.mult).then_inc(sem["b_gp"], 1)
                if ahead:
                    dve.wait_ge(sem["b_xn"], f + 1)
                    if isinstance(f, int) and f == G - 2:
                        dve.wait_ge(sem["a_x1"], G)
                    row_stats(f + 1)
                if has(m):
                    gated(0)
                    gated(1)
                if has(t):
                    dve.wait_ge(sem["b_gp"], t + 1)
                    dve.wait_ge(sem["b_s"], t + 1)
                    after(dve, sem["b_sgT"], t)
                    v.scalar_tensor_tensor(sg[:, :], q_S[:, :], fac[:, F_FAC:F_FAC + 1], gp[:, :], ALU.mult,
                                           ALU.mult).then_inc(sem["b_sg"], 1)
                if has(f):
                    for tap in range(TAPS - 1):
                        conv(f, 0, tap)
                if has(f):
                    lp = q_Q[:, 0:J * NR].rearrange("p (j r) -> p j r", r=NR)
                    if ahead:
                        dve.wait_ge(sem["bn_done"], G + f + 2)
                    dve.wait_ge(sem["b_rout"], f + 1)
                    v.tensor_reduce(mx[:, :], lp, AX.X, ALU.max).then_inc(sem["b_mx"], 1)
                    dve.wait_ge(sem["b_mx"], f + 1)
                    after(dve, sem["b_pe"], f)
                    v.tensor_tensor(lg[:, :, :], lp, mx[:, :].unsqueeze(2).to_broadcast([P, J, NR]),
                                    ALU.subtract).then_inc(sem["b_lg"], 1)
                if ahead:
                    row_moments(sem["b_stat"])
                if has(m):
                    cap(0)
                    gated(2)
                if has(f):
                    conv(f, 1, 0)
                if has(m):
                    cap(1)
                if has(f):
                    conv(f, 1, 1)
                if has(m):
                    softplus(0)
                    softplus(1)
                    gated(3)
                if has(f):
                    conv(f, 1, 2)
                if has(m):
                    output_weight(0)
                    gated(4)
                    output_weight(1)
                if has(t):
                    dve.wait_ge(sem["b_sgT"], t + 1)
                    v.tensor_tensor(xs_of(t), xs_of(t), q_Q[:, :], ALU.add).then_inc(sem["b_out"], 1)
                if has(f):
                    residual(0)
                if has(m):
                    gated(5)
                if has(f):
                    residual(1)
                if has(m):
                    dve.wait_ge(sem["b_b"], m + 1)
                    for k in range(IC):
                        v.scalar_tensor_tensor(bx[:, k, :], q_T[:, :], fac[:, B_FAC:B_FAC + 1], xc2[:, k, :],
                                               ALU.mult, ALU.mult).then_inc(sem["b_bx"], 1)
                    gated(6)
                    state(0)
                if has(f):
                    activated(0)
                if has(m):
                    gated(7)
                    state(1)
                if has(f):
                    activated(1)
                    top_four(f)
                    gates(f)
                if ahead:
                    turned_low(f + 1)

            bodies(dve, layer1)

        @block.tensor
        def _(pe):
            def mm(ps, lhsT, rhs, start=True, stop=True):
                return nc.tensor.matmul(ps, lhsT, rhs, start=start, stop=stop)

            def split3(ps, wh, wl, h, l):
                mm(ps, wh, h, True, False)
                mm(ps, wh, l, False, False)
                return mm(ps, wl, h, False, True)

            def turn_rows(ps):
                for j in range(J):
                    last = nc.tensor.transpose(ps[:, j::J], xn[:, j, :], ident[:, :])
                return last

            def turn_back(ps):
                for j in range(J):
                    last = nc.tensor.transpose(ps[:, j * P:(j + 1) * P], sg[:, j::J], ident[:, :])
                return last

            pe.wait_ge(sem["wq_loaded"], WQ_ALL)
            pe.wait_ge(sem["ident_ready"], 1)
            for i in range(4):
                last = nc.tensor.transpose(b_S[:, i * P:(i + 1) * P], wsq[:, i, :], ident[:, :])
            last.then_inc(sem["square_turned"], 1)

            def layer0(n):
                f, m, t = n, n - 1, n - 2

                def hidden0(j):
                    if j < 2:
                        pe.wait_ge(sem[("a_ek", "a_kv")[j]], f + 1)
                    elif has(m):
                        pe.wait_ge(sem["a_lo1"], (FC - POOLED) * m + j - POOLED + 1)
                    mm(b_Z[0][j][:, :], w0[:, j * P:(j + 1) * P], xh[:, :], True, False)
                    mm(b_Z[0][j][:, :], w0[:, j * P:(j + 1) * P], xl[:, :], False, True).then_inc(sem["a_z0"], 1)

                def hidden1(j):
                    if j < 2:
                        pe.wait_ge(sem["a_lo0"], FC * m + FC)
                    else:
                        pe.wait_ge(sem["a_relu"], POOLED * m + j - 1)
                    for k in range(FC):
                        w = w1[:, k, j * P:(j + 1) * P]
                        mm(b_Z[1][j][:, :], w, hh[:, 0, k, :], k == 0, False)
                        last = mm(b_Z[1][j][:, :], w, hl[:, 0, k, :], False, k == FC - 1)
                    last.then_inc(sem["a_z1"], 1)

                if has(f):
                    pe.wait_ge(sem["a_xn"], f + 1)
                    after(pe, sem["a_xl"], f)
                    turn_rows(b_T).then_inc(sem["a_xnT"], 1)
                if has(m):
                    if isinstance(m, int) and m == 0:
                        pe.wait_ge(sem["w1_ready"], 2)
                    hidden1(0)
                if has(t):
                    pe.wait_ge(sem["a_sg"], t + 1)
                    pe.wait_ge(sem["a_thr"], at_most(t + 2))
                    turn_back(b_RX).then_inc(sem["a_sgT"], 1)
                if has(m):
                    hidden1(1)
                if has(f):
                    pe.wait_ge(sem["a_xm"], f + 1)
                    if isinstance(f, int) and f == 0:
                        pe.wait_ge(sem["square_ready"], 1)
                    after(pe, sem["a_ek"], f)
                    mm(b_K[:, :], wsqT[:, 0, :], xm[:, :]).then_inc(sem["a_k"], 1)
                    after(pe, sem["a_kv"], f)
                    mm(b_V[:, :], wsqT[:, 1, :], xm[:, :]).then_inc(sem["a_v"], 1)
                if has(m):
                    hidden1(2)
                    hidden1(3)
                if has(f):
                    if has(t):
                        pe.wait_ge(sem["a_x1"], t + 1)
                    mm(b_RX[:, :], wsqT[:, 2, :], xm[:, :]).then_inc(sem["a_r"], 1)
                    pe.wait_ge(sem["a_xl"], f + 1)
                    if isinstance(f, int) and f == 0:
                        pe.wait_ge(sem["const_done"], 1)
                    for j in range(FC):
                        hidden0(j)
                if has(m):
                    after(pe, sem["a_gp"], m)
                    for k in range(FC):
                        if k < POOLED:
                            pe.wait_ge(sem["a_low"], POOLED * m + k + 1)
                        else:
                            pe.wait_ge(sem["a_lo1"], (FC - POOLED) * m + k - POOLED + 1)
                        mm(b_F[:, :], w2[:, k, :], hh[:, 1, k, :], k == 0, False)
                        last = mm(b_F[:, :], w2[:, k, :], hl[:, 1, k, :], False, k == FC - 1)
                    last.then_inc(sem["a_f"], 1)
                if has(m):
                    pe.wait_ge(sem["a_y"], m + 1)
                    after(pe, sem["a_sg"], m)
                    mm(b_S[:, :], wsqT[:, 3, :], ya[:, :]).then_inc(sem["a_s"], 1)

            def weights():
                pe.wait_ge(sem["b_xn"], 1)
                turn_rows(q_T).then_inc(sem["b_xnT"], 1)
                for i, batch in enumerate(batches):
                    if i >= 2:
                        pe.wait_ge(sem["prep_out"], i - 1)
                    col = 0
                    for src, width in batch:
                        rows, cols = src.shape[0], src.shape[1]
                        last = nc.tensor.transpose((b_K, b_V)[i % 2][0:cols, col:col + rows], src, ident[0:rows, 0:rows])
                        col += rows
                    last.then_inc(sem["prep_turned"], 1)
                pe.wait_ge(sem["prep_out"], NB)
                for k in range(IC):
                    last = mm((b_K, b_V)[NB % 2][:, k * DI:(k + 1) * DI], wxsT[:, k, :], wdt[:, :])
                last.then_inc(sem["prep_turned"], 1)

            bodies(pe, layer0, {G: weights})

            def xc_product(ps, wh, wl, i):
                w = slice(i * P, (i + 1) * P)
                for k in range(IC):
                    mm(ps[:, :], wh[:, k, w], xch[:, k, :], k == 0, False)
                    mm(ps[:, :], wh[:, k, w], xcl[:, k, :], False, False)
                    last = mm(ps[:, :], wl[:, k, w], xch[:, k, :], False, k == IC - 1)
                return last

            def layer1(n):
                f, m, t = n, n - 1, n - 2

                def product_in(ps, i):
                    w = slice(i * P, (i + 1) * P)
                    return split3(ps[:, :], w_inH[:, w], w_inL[:, w], xh[:, :], xl[:, :])

                def conv_in(i):
                    if has(m):
                        pe.wait_ge(sem["b_act"], UC * m + UC)
                    product_in(q_U[i], i).then_inc(sem["b_xin"], 1)

                def residual_in(i):
                    if has(m):
                        pe.wait_ge(sem["b_xdt"], IC * m + i + 1)
                    product_in((q_T, q_S)[i], IC + i).then_inc(sem["b_res"], 1)

                def steps(i):
                    if i:
                        after(pe, sem["b_sg"], m)
                    elif not has(f):
                        after(pe, sem["b_bx"], IC * m)
                    xc_product((q_T, q_S)[i], wdH, wdL, i).then_inc(sem["b_d"], 1)

                def output_weights(i):
                    if has(f):
                        pe.wait_ge(sem["b_u0"], IC * f + i + 1)
                    else:
                        pe.wait_ge(sem["b_act"], UC * m + UC)
                    xc_product(q_U[i], wcH, wcL, i).then_inc(sem["b_c"], 1)

                def spread(c):
                    after(pe, sem["b_actg"], RC * m + c - 1 if c else RC * m)
                    mm(q_D[c % 2][:, :], sel[:, c, :], gT[:, :]).then_inc(sem["b_gate"], 1)

                def expert_in(c):
                    if c >= 2:
                        pe.wait_ge(sem["b_act"], UC * f + c - 1)
                    elif has(m):
                        pe.wait_ge(sem["b_cr"], IC * m + c + 1)
                    else:
                        pe.wait_ge(sem["b_u0"], IC * f + c + 1)
                    w = slice(c * P, (c + 1) * P)
                    split3(q_U[c % 2][:, :], upH[:, w], upL[:, w], xh[:, :], xl[:, :]).then_inc(sem["b_up"], 1)

                def expert_out(c):
                    if c:
                        pe.wait_ge(sem["b_low"], RC * m + c)
                    else:
                        pe.wait_ge(sem["b_low0"], m + 1)
                        after(pe, sem["b_gp"], m)
                    h, l = (ph[:, (c - 1) % RING, :], pl[:, (c - 1) % RING, :]) if c else (s0h[:, :], s0l[:, :])
                    w = slice(c * P, (c + 1) * P)
                    mm(q_F[:, :], dnH[:, w], h, c == 0, False)
                    mm(q_F[:, :], dnL[:, w], h, False, False)
                    mm(q_F[:, :], dnH[:, w], l, False, c == UC - 1).then_inc(sem["b_down"], 1)

                if has(f):
                    pe.wait_ge(sem["b_xl"], f + 1)
                    conv_in(0)
                if has(m):
                    pe.wait_ge(sem["b_xcl"], IC * m + IC)
                    steps(0)
                    pe.wait_ge(sem["b_gT"], m + 1)
                    spread(0)
                    spread(1)
                if has(f):
                    conv_in(1)
                    for j in range(J):
                        ps = q_Q[:, j * NR:(j + 1) * NR]
                        mm(ps, xh[:, j::J], rwH[:, :], True, False)
                        mm(ps, xl[:, j::J], rwH[:, :], False, False)
                        last = mm(ps, xh[:, j::J], rwL[:, :], False, True)
                    last.then_inc(sem["b_rout"], 1)
                if has(m):
                    steps(1)
                    expert_out(0)
                    spread(2)
                    output_weights(0)
                    spread(3)
                if has(t):
                    pe.wait_ge(sem["b_sg"], t + 1)
                    if has(f):
                        pe.wait_ge(sem["b_lg"], f + 1)
                    elif has(m):
                        pe.wait_ge(sem["b_gT"], m + 1)
                    else:
                        pe.wait_ge(sem["b_out"], t)
                    turn_back(q_Q).then_inc(sem["b_sgT"], 1)
                if has(m):
                    expert_out(1)
                    output_weights(1)
                if has(f):
                    residual_in(0)
                if has(m):
                    spread(4)
                    expert_out(2)
                if has(f):
                    residual_in(1)
                    expert_in(0)
                if has(m):
                    spread(5)
                    expert_out(3)
                    if has(f):
                        pe.wait_ge(sem["b_r2"], IC * f + 1)
                    else:
                        pe.wait_ge(sem["b_xdt"], IC * m + 1)
                    xc_product(q_T, wbH, wbL, 0).then_inc(sem["b_b"], 1)
                if has(f):
                    expert_in(1)
                if has(m):
                    spread(6)
                    expert_out(4)
                if has(f):
                    expert_in(2)
                if has(m):
                    spread(7)
                    expert_out(5)
                if has(f):
                    expert_in(3)
                    expert_in(4)
                if has(m):
                    expert_out(6)
                if has(f):
                    expert_in(5)
                if has(f) and has(f + 1):
                    pe.wait_ge(sem["b_xn"], f + 2)
                    if has(m):
                        pe.wait_ge(sem["b_bx"], IC * m + IC)
                    else:
                        pe.wait_ge(sem["b_r2"], IC * f + 1)
                    turn_rows(q_T).then_inc(sem["b_xnT"], 1)
                if has(m):
                    expert_out(7)
                if has(f):
                    expert_in(6)
                    expert_in(7)
                    expert_in(8)
                if has(m):
                    expert_out(8)
                    pe.wait_ge(sem["b_y"], IC * m + IC)
                    if has(f):
                        pe.wait_ge(sem["b_r2"], IC * f + IC)
                    else:
                        pe.wait_ge(sem["b_xdt"], IC * m + IC)
                    for k in range(IC):
                        if has(f) and k == IC - 1:
                            pe.wait_ge(sem["b_g4"], f + 1)
                            if has(t):
                                pe.wait_ge(sem["b_out"], t + 1)
                        last = mm(q_S[:, :], w_out[:, k, :], yb[:, k, :], k == 0, k == IC - 1)
                    last.then_inc(sem["b_s"], 1)
                if has(f):
                    if not has(m):
                        pe.wait_ge(sem["b_g4"], f + 1)
                    gps = q_Q[0:3 * NR, 0:N // 2].bitcast(BF16)
                    for j in range(J):
                        last = nc.tensor.transpose(gps[:, j * P:(j + 1) * P], g3[:, j, :, :].rearrange("p a r -> p (a r)"),
                                                   identb[:, :])
                    last.then_inc(sem["b_gtT"], 1)

            pe.wait_ge(sem["a_x1"], G)
            pe.wait_ge(sem["prep_out"], NB + 1)
            pe.wait_ge(sem["prep_sbuf"], 1)
            pe.wait_ge(sem["ident_ready"], 2)
            pe.wait_ge(sem["sel_ready"], 4)
            bodies(pe, layer1)


_INS = ["L0_attn_x", "L0_attn_time_decay", "L0_attn_time_first", "L0_attn_time_mix", "L0_attn_Wk", "L0_attn_Wv",
        "L0_attn_Wr", "L0_attn_Wo", "L0_ffn_k0", "L0_ffn_k1", "L0_ffn_k2", "L0_ffn_s0", "L0_ffn_s1", "L0_ffn_s2",
        "L1_attn_W_in", "L1_attn_conv_w", "L1_attn_conv_b", "L1_attn_W_x", "L1_attn_W_dt", "L1_attn_b_dt",
        "L1_attn_W_out", "L1_ffn_shared_up", "L1_ffn_shared_down", "L1_ffn_routed_up", "L1_ffn_routed_down",
        "L1_ffn_router_w"]


def kernel(**inputs):
    import numpy as _np
    import concourse.bacc as _bacc
    from concourse import mybir as _mybir
    from concourse.bass_utils import run_bass_kernel_spmd as _run

    nc = _bacc.Bacc("TRN2", target_bir_lowering=False, num_devices=1)
    arrays, args = {}, {}
    for name in _INS:
        a = _np.ascontiguousarray(inputs[name])
        if a.ndim == 0:
            a = a.reshape(1)
        arrays[f"in_{name}"] = a
        args[name] = nc.dram_tensor(f"in_{name}", a.shape, _mybir.dt.from_np(a.dtype), kind="ExternalInput").ap()
    out = nc.dram_tensor("out_0", inputs["L0_attn_x"].shape, F32, kind="ExternalOutput").ap()
    build(nc, args, out)
    r = _run(nc, [arrays], core_ids=[0])
    return r.results[0]["out_0"]
```
